# Optimizing a Trainium2 kernel written in Bass

```python
import numpy as np
import jax
import jax.numpy as jnp

def _softmax(x, axis=-1):
    return jax.nn.softmax(x, axis=axis)

def _gelu(x):
    return jax.nn.gelu(x, approximate=True)

def _silu(x):
    return jax.nn.silu(x)

def _sigmoid(x):
    return jax.nn.sigmoid(x)

def _layernorm(x, axis=-1, eps=1e-05):
    m = jnp.mean(x, axis=axis, keepdims=True)
    v = jnp.var(x, axis=axis, keepdims=True)
    return (x - m) / jnp.sqrt(v + eps)

def _scatter_add(tgt, idx, src, axis=0):
    return tgt.at[idx].add(src)

def _segment_sum(src, seg, n):
    return jax.ops.segment_sum(src, seg, n)
kernel_name = 'mk_gnn_resnorm_d4_gnn_r8_17baaa'

def setup_inputs(seed: int=0):
    np.random.seed(seed)
    _w = jnp.asarray

    def _rec_inputs():
        import jax
        import jax.numpy as jnp
        _gk = jax.random.key(seed)
        x = -0.000202 + 1 * jax.random.normal(jax.random.fold_in(_gk, 1), (12500, 64), jnp.float32)
        src = jax.random.randint(jax.random.fold_in(_gk, 2), (400000,), 0, 12500, jnp.int32)
        dst = jnp.minimum((12500 * jax.random.uniform(jax.random.fold_in(_gk, 3), (400000,)) ** 2.0).astype(jnp.int32), 99999)
        _o = jnp.argsort(dst, stable=True)
        src = src[_o]
        dst = dst[_o]
        edge_attr_16 = -5.3897e-05 + 0.999841 * jax.random.normal(jax.random.fold_in(_gk, 12), (400000, 16), jnp.float32)
        edge_type_16 = jax.random.randint(jax.random.fold_in(_gk, 14), (400000,), 0, 16, jnp.int32)
        edge_weight1 = jax.random.uniform(jax.random.fold_in(_gk, 15), (400000, 1), jnp.float32, 0.0, 1)
        return (x, src, dst, edge_attr_16, edge_type_16, edge_weight1)
    x, src, dst, edge_attr_16, edge_type_16, edge_weight1 = _rec_inputs()

    def _L0_gnn_setup():
        import jax, jax.numpy as jnp
        import numpy as np
        N_NODES = 12500
        N_EDGES = 156250
        IN_FEAT = 64
        OUT_FEAT = 64
        key = jax.random.key(seed)
        k_h, k_w, k_src, k_dst, k_W, k_b = jax.random.split(key, 6)
        h = jax.random.normal(k_h, (N_NODES, IN_FEAT), dtype=jnp.float32)
        w = jax.random.uniform(k_w, (N_EDGES, 1), dtype=jnp.float32)
        src = jax.random.randint(k_src, (N_EDGES,), 0, N_NODES, dtype=jnp.int64 if jax.config.jax_enable_x64 else jnp.int32)
        dst = jax.random.randint(k_dst, (N_EDGES,), 0, N_NODES, dtype=jnp.int64 if jax.config.jax_enable_x64 else jnp.int32)
        W = jax.random.normal(k_W, (OUT_FEAT, 2 * IN_FEAT), dtype=jnp.float32) * 0.05
        b = jax.random.normal(k_b, (OUT_FEAT,), dtype=jnp.float32) * 0.05
        return {'h': h, 'w': w, 'src': src, 'dst': dst, 'W': W, 'b': b}
    _L0_gnn_all = _L0_gnn_setup()
    _L0_gnn_in = {k: v for k, v in _L0_gnn_all.items() if k in ('W', 'b')}
    del _L0_gnn_all

    def _L1_gnn_setup():
        import jax, jax.numpy as jnp
        import numpy as np
        N_NODES = 6250
        N_EDGES = 200000
        D_NODE = 64
        D_EDGE = 16
        HEADS = 4
        ATT_F = 16
        LN_EPS = 1e-06
        key = jax.random.key(seed)
        ks = jax.random.split(key, 9)
        nodes = jax.random.normal(ks[0], (N_NODES, D_NODE), dtype=jnp.float32)
        edges = jax.random.normal(ks[1], (N_EDGES, D_EDGE), dtype=jnp.float32)
        receivers = jax.random.randint(ks[2], (N_EDGES,), 0, N_NODES)
        senders = jax.random.randint(ks[3], (N_EDGES,), 0, N_NODES)
        W = jax.random.normal(ks[4], (HEADS, ATT_F, D_NODE), dtype=jnp.float32) * np.sqrt(2.0 / D_NODE)
        W_edge = jax.random.normal(ks[5], (HEADS, ATT_F, D_EDGE), dtype=jnp.float32) * np.sqrt(2.0 / D_EDGE)
        a = jax.random.normal(ks[6], (HEADS, 3 * ATT_F), dtype=jnp.float32) * np.sqrt(2.0 / (HEADS + 3 * ATT_F))
        ln_scale = jnp.ones((HEADS * ATT_F,), dtype=jnp.float32)
        ln_bias = jnp.zeros((HEADS * ATT_F,), dtype=jnp.float32)
        return {'nodes': nodes, 'edges': edges, 'receivers': receivers, 'senders': senders, 'W': W, 'W_edge': W_edge, 'a': a, 'ln_scale': ln_scale, 'ln_bias': ln_bias}
    _L1_gnn_all = _L1_gnn_setup()
    _L1_gnn_in = {k: v for k, v in _L1_gnn_all.items() if k in ('W', 'W_edge', 'a', 'ln_scale', 'ln_bias')}
    del _L1_gnn_all

    def _L2_gnn_setup():
        import jax, jax.numpy as jnp
        import numpy as np
        N_NODES = 6250
        N_EDGES = 100000
        D_IN = 64
        D_OUT = 64
        NUM_RELS = 16
        key = jax.random.key(seed)
        k1, k2, k3, k4, k5 = jax.random.split(key, 5)
        feat = jax.random.normal(k1, (N_NODES, D_IN), dtype=jnp.float32)
        weight = jax.random.normal(k2, (NUM_RELS, D_IN, D_OUT), dtype=jnp.float32) * 0.05
        src = jax.random.randint(k3, (N_EDGES,), 0, N_NODES, dtype=jnp.int32)
        dst = jax.random.randint(k4, (N_EDGES,), 0, N_NODES, dtype=jnp.int32)
        etypes = jax.random.randint(k5, (N_EDGES,), 0, NUM_RELS, dtype=jnp.int32)
        return {'feat': feat, 'weight': weight, 'src': src, 'dst': dst, 'etypes': etypes}
    _L2_gnn_all = _L2_gnn_setup()
    _L2_gnn_in = {k: v for k, v in _L2_gnn_all.items() if k in ('weight',)}
    del _L2_gnn_all

    def _L3_gnn_setup():
        import jax, jax.numpy as jnp
        import numpy as np
        N = 12500
        D = 64
        DEG = 16
        H = 2
        ALPHA = 0.2
        key = jax.random.key(seed)
        k1, k2, k3 = jax.random.split(key, 3)
        inputs = jax.random.normal(k1, (N, D), dtype=jnp.float32)
        rnd = jax.random.randint(k2, (2, N * DEG), 0, N)
        self_loops = jnp.tile(jnp.arange(N)[None, :], (2, 1))
        edge_index = jnp.concatenate([self_loops, rnd], axis=1)
        W = jnp.ones((H, D), dtype=jnp.float32)
        stdv = 1.0 / np.sqrt(D * 2)
        a = jax.random.uniform(k3, (H, 2 * D), dtype=jnp.float32, minval=-stdv, maxval=stdv)
        return {'inputs': inputs, 'edge_index': edge_index, 'W': W, 'a': a}
    _L3_gnn_all = _L3_gnn_setup()
    _L3_gnn_in = {k: v for k, v in _L3_gnn_all.items() if k in ('W', 'a')}
    del _L3_gnn_all
    return {'x': x, 'src': src, 'dst': dst, 'edge_attr_16': edge_attr_16, 'edge_type_16': edge_type_16, 'edge_weight1': edge_weight1, 'L0_gnn_W': _L0_gnn_in['W'], 'L0_gnn_b': _L0_gnn_in['b'], 'L1_gnn_W': _L1_gnn_in['W'], 'L1_gnn_W_edge': _L1_gnn_in['W_edge'], 'L1_gnn_a': _L1_gnn_in['a'], 'L1_gnn_ln_scale': _L1_gnn_in['ln_scale'], 'L1_gnn_ln_bias': _L1_gnn_in['ln_bias'], 'L2_gnn_weight': _L2_gnn_in['weight'], 'L3_gnn_W': _L3_gnn_in['W'], 'L3_gnn_a': _L3_gnn_in['a']}

def reference(x, src, dst, edge_attr_16, edge_type_16, edge_weight1, L0_gnn_W, L0_gnn_b, L1_gnn_W, L1_gnn_W_edge, L1_gnn_a, L1_gnn_ln_scale, L1_gnn_ln_bias, L2_gnn_weight, L3_gnn_W, L3_gnn_a):
    import jax
    import jax.numpy as jnp

    def _L0_gnn_ref(h, w, src, dst, W, b):
        import jax, jax.numpy as jnp
        import numpy as np
        N_NODES = 12500
        N_EDGES = 156250
        IN_FEAT = 64
        OUT_FEAT = 64
        m = h[src] * w
        agg = jax.ops.segment_sum(m, dst, num_segments=N_NODES)
        cnt = jax.ops.segment_sum(jnp.ones((m.shape[0],), m.dtype), dst, num_segments=N_NODES)
        h_neigh = agg / jnp.maximum(cnt, 1.0)[:, None]
        h_total = jnp.concatenate([h, h_neigh], axis=1)
        return jax.nn.relu(h_total @ W.T + b)

    def _L1_gnn_ref(nodes, edges, receivers, senders, W, W_edge, a, ln_scale, ln_bias):
        import jax, jax.numpy as jnp
        import numpy as np
        N_NODES = 6250
        N_EDGES = 200000
        D_NODE = 64
        D_EDGE = 16
        HEADS = 4
        ATT_F = 16
        LN_EPS = 1e-06
        n = nodes.shape[0]
        self_idx = jnp.arange(n)
        r = jnp.concatenate([receivers, self_idx], axis=0)
        s = jnp.concatenate([senders, self_idx], axis=0)
        e = jnp.concatenate([edges, jnp.zeros((n, edges.shape[1]), edges.dtype)], axis=0)
        Wn = jnp.einsum('hfi,ni->nhf', W, nodes)
        Ws = Wn[s]
        Wr = Wn[r]
        We = jnp.einsum('hfi,ei->ehf', W_edge, e)
        a_s, a_r, a_e = jnp.split(a, 3, axis=-1)
        msg = jnp.einsum('ehf,hf->eh', Ws, a_s) + jnp.einsum('ehf,hf->eh', Wr, a_r) + jnp.einsum('ehf,hf->eh', We, a_e)
        lm = jax.nn.leaky_relu(msg)
        seg_max = jax.ops.segment_max(lm, r, num_segments=n)
        z = lm - seg_max[r]
        exp_z = jnp.exp(z)
        norm = jax.ops.segment_sum(exp_z, r, num_segments=n)
        alpha = exp_z / norm[r]
        att_msg = alpha[:, :, None] * Ws
        aggr = jax.ops.segment_sum(att_msg, r, num_segments=n)
        out = aggr.reshape(n, -1)
        out = jax.nn.elu(out)
        mean = jnp.mean(out, axis=-1, keepdims=True)
        var = jnp.mean(jnp.square(out - mean), axis=-1, keepdims=True)
        out = (out - mean) * jax.lax.rsqrt(var + LN_EPS)
        out = out * ln_scale + ln_bias
        return out

    def _L2_gnn_ref(feat, weight, src, dst, etypes):
        import jax, jax.numpy as jnp
        import numpy as np
        N_NODES = 6250
        N_EDGES = 100000
        D_IN = 64
        D_OUT = 64
        NUM_RELS = 16
        num_rels = weight.shape[0]
        h_src = feat[src]
        msg = jnp.zeros((h_src.shape[0], weight.shape[2]), dtype=feat.dtype)
        for r in range(num_rels):
            mask = etypes == r
            msg = msg + h_src * mask[:, None].astype(feat.dtype) @ weight[r]
        out = jax.ops.segment_sum(msg, dst, num_segments=feat.shape[0])
        return out

    def _L3_gnn_ref(inputs, edge_index, W, a):
        import jax, jax.numpy as jnp
        import numpy as np
        N = 12500
        D = 64
        DEG = 16
        H = 2
        ALPHA = 0.2
        n = inputs.shape[0]
        row, col = (edge_index[0], edge_index[1])

        def head(Wh, ah):
            h = inputs * Wh
            score = (h @ ah[:D])[row] + (h @ ah[D:])[col]
            e = jnp.exp(jnp.where(score > 0, score, ALPHA * score))
            rowsum = jax.ops.segment_sum(e, row, num_segments=n)
            h_prime = jax.ops.segment_sum(e[:, None] * inputs[col], row, num_segments=n)
            return h_prime / rowsum[:, None]
        outs = jax.vmap(head)(W, a)
        return outs.mean(axis=0)
    edge_index = jnp.stack([src, dst])
    x = _layernorm(x + _L0_gnn_ref(x, edge_weight1, src, dst, L0_gnn_W, L0_gnn_b), axis=-1)
    x = _layernorm(x + _L1_gnn_ref(x, edge_attr_16, dst, src, L1_gnn_W, L1_gnn_W_edge, L1_gnn_a, L1_gnn_ln_scale, L1_gnn_ln_bias), axis=-1)
    x = _layernorm(x + _L2_gnn_ref(x, L2_gnn_weight, src, dst, edge_type_16), axis=-1)
    x = _layernorm(x + _L3_gnn_ref(x, edge_index, L3_gnn_W, L3_gnn_a), axis=-1)
    return x

_drawn_inputs = setup_inputs


def setup_inputs(seed=0):
    import zlib

    import numpy as np

    out = dict(_drawn_inputs(seed))
    spreads = {'L1_gnn_ln_scale': (1.0, 0.2), 'L1_gnn_ln_bias': (0.0, 0.1), 'L3_gnn_W': (1.0, 0.6)}
    factors = {'edge_weight1': 3.954}
    for name, (base, spread) in spreads.items():
        noise = np.random.default_rng([zlib.crc32(name.encode()), seed]).standard_normal(out[name].shape)
        drawn = base * np.exp(spread * noise) if base else spread * noise
        out[name] = jnp.asarray(drawn.astype(out[name].dtype))
    for name, factor in factors.items():
        out[name] = (out[name] * factor).astype(out[name].dtype)
    return out
```

```python
from contextlib import ExitStack

import concourse.bass as bass
from concourse import mybir

ALU = mybir.AluOpType
ACT = mybir.ActivationFunctionType
AX = mybir.AxisListType
F32 = mybir.dt.float32
I32 = mybir.dt.int32
U32 = mybir.dt.uint32

P = 128
NODES, EDGES, D = 12500, 400000, 64
ETYPES, EDIM, HEADS, HF = 16, 16, 4, 16
HEADS3 = 2
TILES = EDGES // P
WINS = -(-NODES // P)
NPAD = WINS * P
TAIL = NODES - (WINS - 1) * P
U, RINGS = 8, 4
QS, GS = 101, 32
STEPS = QS * GS
REAL = TILES + WINS - 1
GROUPS = STEPS // U
TURNS = GROUPS // RINGS
assert TILES * P == EDGES and STEPS >= REAL and GROUPS * U == STEPS and TURNS * RINGS == GROUPS
BIG = 1e30
LN_EPS, LN1_EPS = 1e-5, 1e-6
BLK = 7
BLKS = WINS // BLK
assert BLK * BLKS == WINS
ACCW = D + 2 * HEADS


class Link:

    def __init__(self, eng, sem):
        self.eng, self.sem, self.base, self.n = eng, sem, 0, 0

    def __call__(self, ins):
        self.n += 1
        ins.then_inc(self.sem, 1)
        self.eng.wait_ge(self.sem, self.base + self.n)

    def turn(self, start, i, per):
        self.base, self.n = i * per + start, 0


def bc(ap, axis, n):
    ap = ap.unsqueeze(axis)
    shape = list(ap.shape)
    shape[axis] = n
    return ap.broadcast_to(shape)


def alone(eng):
    eng.nop(nofuse=True)


class Semaphores:

    def __init__(self, nc):
        self.nc, self.ctx, self.given = nc, ExitStack(), []

    def __call__(self, name):
        self.given.append(self.ctx.enter_context(self.nc.semaphore(name)))
        return self.given[-1]

    def clear(self):
        with self.nc.Block() as block:
            @block.sync
            def _(sp):
                for s in self.given:
                    sp.sem_clear(s)
        self.ctx.close()
        self.given = []


class Mem:
    pass


def constants(nc, m):
    with ExitStack() as ctx:
        rowi = ctx.enter_context(nc.sbuf_tensor("rowi", [P, P], I32))
        coli = ctx.enter_context(nc.sbuf_tensor("coli", [P, 1], I32))
        ints_made, consts = m.sem("ints_made"), m.sem("consts")
        block = ctx.enter_context(nc.Block())

        @block.gpsimd
        def _(pool):
            pool.iota(rowi[:], [[1, P]], base=0, channel_multiplier=0).then_inc(ints_made, 1)
            pool.iota(coli[:], [[0, 1]], base=0, channel_multiplier=1).then_inc(ints_made, 1)

        @block.vector
        def _(dve):
            link = Link(dve, consts)
            dve.wait_ge(ints_made, 2)
            link(dve.tensor_copy(m.row[:], rowi[:]))
            link(dve.tensor_copy(m.col[:], coli[:]))
            link(dve.tensor_scalar(m.ident[:], m.row[:], m.col[:, 0:1], None, ALU.is_equal))
            link(dve.tensor_scalar(m.lower[:], m.row[:], m.col[:, 0:1], None, ALU.is_lt))
            link(dve.tensor_scalar(m.trash[:], m.col[:], float(NPAD), None, ALU.add))


def schedule(nc, m, dst):
    with ExitStack() as ctx:
        def sb(name, shape, dt=F32):
            return ctx.enter_context(nc.sbuf_tensor(name, shape, dt))

        T = WINS - 1
        lasti, lastf = sb("lasti", [T, TILES], I32), sb("lastf", [T, TILES])
        below, limit, move = sb("below", [T, TILES]), sb("limit", [T, 1]), sb("move", [T, 1])
        moves = sb("moves", [QS, T])
        kint, kf = sb("kint", [QS, GS], I32), sb("kf", [QS, GS])
        past = sb("past", [QS, GS, T])
        win, void, tile = sb("win", [QS, GS]), sb("void", [QS, GS]), sb("tile", [QS, GS])
        wini = sb("wini", [QS, GS], I32)
        last_d = nc.dram_tensor("last_d", [TILES], I32, kind="Internal").ap()
        move_d = nc.dram_tensor("move_d", [T], F32, kind="Internal").ap()
        win_d = nc.dram_tensor("win_d", [STEPS], I32, kind="Internal").ap()
        s_last, s_lastb, s_k, s_move, s_moves, s_wini, s_dve, s_win = [m.sem(n) for n in (
            "last_out", "last_in", "k_made", "move_out", "moves_in", "win_out", "sched_chain", "winrow_in")]
        n_move, n_win = 5, 15
        block = ctx.enter_context(nc.Block())

        @block.gpsimd
        def _(pool):
            pool.iota(kint[:], [[QS, GS]], base=0, channel_multiplier=1).then_inc(s_k, 1)

        @block.sync
        def _(sp):
            with nc.allow_non_contiguous_dma(reason="the last dst of each tile, once"):
                sp.dma_start(last_d.rearrange("(a b) -> a b", b=5),
                             dst.rearrange("(a b p) -> a b p", b=5, p=P)[:, :, P - 1]).then_inc(s_last, 16)
                sp.wait_ge(s_last, 16)
                sp.dma_start(lasti[:], last_d.unsqueeze(0).broadcast_to([T, TILES])).then_inc(s_lastb, 16)
                sp.wait_ge(s_dve, n_move)
                sp.dma_start(move_d.unsqueeze(1), move[:]).then_inc(s_move, 16)
                sp.wait_ge(s_move, 16)
                sp.dma_start(moves[:], move_d.unsqueeze(0).broadcast_to([QS, T])).then_inc(s_moves, 16)
                sp.wait_ge(s_dve, n_win)
                sp.dma_start(win_d.rearrange("(g q) -> q g", q=QS), wini[:]).then_inc(s_wini, 16)
                sp.wait_ge(s_wini, 16)
                sp.dma_start(m.winrow[0:1, :], win_d.unsqueeze(0)).then_inc(s_win, 16)
                sp.wait_ge(s_win, 16)

        @block.vector
        def _(dve):
            link = Link(dve, s_dve)
            link(dve.tensor_scalar(limit[:], m.col[0:T, :], float(P), float(P), ALU.mult, ALU.add))
            dve.wait_ge(s_lastb, 16)
            link(dve.tensor_copy(lastf[:], lasti[:]))
            link(dve.tensor_scalar(below[:], lastf[:], limit[:, 0:1], None, ALU.is_lt))
            link(dve.reduce_sum(move[:], below[:], AX.X))
            link(dve.tensor_scalar(move[:], move[:], float(TILES - 1), m.col[0:T, 0:1], ALU.min, ALU.add))
            assert link.n == n_move
            dve.wait_ge(s_k, 1)
            link(dve.tensor_copy(kf[:], kint[:]))
            dve.wait_ge(s_moves, 16)
            link(dve.tensor_tensor(past[:], bc(moves[:], 1, GS), bc(kf[:], 2, T), ALU.is_lt))
            link(dve.reduce_sum(win[:], past[:], AX.X))
            link(dve.tensor_tensor(tile[:], kf[:], win[:], ALU.subtract))
            link(dve.tensor_scalar(tile[:], tile[:], float(TILES - 1), None, ALU.min))
            link(dve.tensor_copy(m.tileq[:], tile[:]))
            link(dve.tensor_scalar(void[:], kf[:], float(REAL), 1e6, ALU.is_ge, ALU.mult))
            link(dve.tensor_scalar(m.base[:], win[:], float(P), None, ALU.mult))
            link(dve.tensor_tensor(m.base[:], m.base[:], void[:], ALU.add))
            link(dve.tensor_copy(wini[:], win[:]))
            assert link.n == n_win


def step_tables(nc, m, src, dst, etype, w):
    with ExitStack() as ctx:
        def sb(name, shape, dt=F32):
            return ctx.enter_context(nc.sbuf_tensor(name, shape, dt))

        at = sb("at", [QS, 1], U32)
        rows = [sb(f"rows_{n}", [QS, P], dt) for n, dt in (("src", I32), ("dst", I32), ("etype", I32), ("w", F32))]
        srcf, dstf, etf, rel, lo, hi, key, relrow = [sb(n, [QS, P]) for n in (
            "srcf", "dstf", "etf", "rel", "lo", "hi", "key", "relrow")]
        pen = sb("pen", [QS, P + 1])
        first, last = sb("first", [QS, GS]), sb("last", [QS, GS])
        tabs = [sb("t_src", [P, STEPS], U32), sb("t_rel", [P, STEPS], U32), sb("t_w", [P, STEPS]), sb("t_key", [P, STEPS])]
        pt = ctx.enter_context(nc.psum_tensor("pt", [P, 4, 512], F32))
        s_at, s_rows, s_conv, s_pt, s_copied, s_pen, s_out = [m.sem(n) for n in (
            "at_staged", "rows_in", "tab_chain", "tab_turned", "tab_copied", "pen_out", "tabs_out")]
        PER = 14
        block = ctx.enter_context(nc.Block())

        @block.scalar
        def _(act):
            def stage(g):
                act.copy(at[:], m.tileq[:, bass.ds(g, 1)]).then_inc(s_at, 1)
            stage(0)
            with act.Fori(1, GS) as g:
                act.wait_ge(s_rows, g * 64)
                alone(act)
                stage(g)

        @block.gpsimd
        def _(pool):
            def gather():
                for r, t in zip(rows, (src, dst, etype, w.rearrange("e a -> (e a)"))):
                    pool.indirect_dma_start(r[:], None, t.rearrange("(t p) -> t p", p=P),
                                            bass.IndirectOffsetOnAxis(at[:, 0:1], 0)).then_inc(s_rows, 16)
            pool.wait_ge(s_at, 1)
            gather()
            with pool.Fori(1, GS) as g:
                pool.wait_ge(s_at, g + 1)
                pool.wait_ge(s_pt, g)
                alone(pool)
                gather()

        @block.vector
        def _(dve):
            link = Link(dve, s_conv)

            def turn(g, first_turn):
                link.turn(0, g, PER)
                dve.wait_ge(s_rows, g * 64 + 64)
                if not first_turn:
                    dve.wait_ge(s_pt, g)
                    dve.wait_ge(s_pen, g * 16)
                link(dve.tensor_copy(srcf[:], rows[0][:]))
                link(dve.tensor_copy(dstf[:], rows[1][:]))
                link(dve.tensor_copy(etf[:], rows[2][:]))
                link(dve.scalar_tensor_tensor(out=relrow[:], in0=srcf[:], scalar=float(ETYPES), in1=etf[:],
                                              op0=ALU.mult, op1=ALU.add))
                link(dve.tensor_scalar(rel[:], dstf[:], m.base[:, bass.ds(g, 1)], None, ALU.subtract))
                link(dve.tensor_scalar(lo[:], rel[:], 0.0, None, ALU.is_ge))
                link(dve.tensor_scalar(hi[:], rel[:], float(P), None, ALU.is_lt))
                link(dve.tensor_tensor(lo[:], lo[:], hi[:], ALU.mult))
                link(dve.scalar_tensor_tensor(out=key[:], in0=rel[:], scalar=1.0, in1=lo[:], op0=ALU.add, op1=ALU.mult))
                link(dve.tensor_scalar(key[:], key[:], -1.0, None, ALU.add))
                link(dve.tensor_tensor(pen[:, 1:P], key[:, 1:P], key[:, 0:P - 1], ALU.not_equal))
                link(dve.tensor_scalar(pen[:, 1:P], pen[:, 1:P], -BIG, None, ALU.mult))
                alone(dve)
                link(dve.tensor_copy(first[:, bass.ds(g, 1)], key[:, 0:1]))
                alone(dve)
                link(dve.tensor_copy(last[:, bass.ds(g, 1)], key[:, P - 1:P]))
                assert link.n == PER
                dve.wait_ge(s_pt, g + 1)
                alone(dve)
                for t, tab in enumerate(tabs):
                    ins = dve.tensor_copy(tab[:, bass.ds(g * QS, QS)], pt[:, t, 0:QS])
                ins.then_inc(s_copied, 1)

            dve.memset(pen[:], 0.0).then_inc(s_copied, 1)
            dve.wait_ge(s_copied, 1)
            turn(0, True)
            with dve.Fori(1, GS) as g:
                turn(g, False)

        @block.tensor
        def _(pe):
            def turn(g, first_turn):
                pe.wait_ge(s_conv, g * PER + PER)
                if not first_turn:
                    pe.wait_ge(s_copied, g + 1)
                for t, r in enumerate((srcf, relrow, rows[3], key)):
                    ins = pe.transpose(pt[:, t, 0:QS], r[:], m.ident[0:QS, 0:QS])
                ins.then_inc(s_pt, 1)
            turn(0, True)
            with pe.Fori(1, GS) as g:
                turn(g, False)

        @block.sync
        def _(sp):
            with sp.Fori(0, GS) as g:
                sp.wait_ge(s_conv, g * PER + PER)
                sp.dma_start(m.pen_d[bass.ds(g, 1)].rearrange("o q p -> (o q) p"), pen[:]).then_inc(s_pen, 16)
            sp.wait_ge(s_copied, GS + 1)
            for d, t in ((m.src_d, tabs[0]), (m.rel_d, tabs[1]), (m.w_d, tabs[2]), (m.key_d, tabs[3])):
                sp.dma_start(d, t[:]).then_inc(s_out, 16)
            with nc.allow_non_contiguous_dma(reason="one key a step"):
                for d, t in ((m.first_d, first), (m.last_d, last)):
                    sp.dma_start(d.rearrange("(g q) -> q g", q=QS), t[:]).then_inc(s_out, 16)
            sp.wait_ge(s_pen, 16 * GS)
            sp.wait_ge(s_out, 6 * 16)


def onehots(dve, m, oh, keys, link_to, u=U):
    for s in range(u):
        ins = dve.tensor_scalar(oh[:, s, :], m.row[:], keys[:, s:s + 1], None, ALU.is_equal)
    ins.then_inc(link_to, 1)


def turns(eng, body, n_turns=TURNS):
    for r in range(RINGS):
        body(r, r, True, False)
    with eng.Fori(1, n_turns - 1) as i:
        for r in range(RINGS):
            body(i * RINGS + r, r, False, False)
    for r in range(RINGS):
        body((n_turns - 1) * RINGS + r, r, False, True)


def after(first, back, r):
    return not (first and r < back)


def sum_pass(nc, m, name, table, idx_d, weighted):
    W = D + 1 if weighted else D
    with ExitStack() as ctx:
        def sb(n, shape, dt=F32):
            return ctx.enter_context(nc.sbuf_tensor(f"{name}_{n}", shape, dt))

        idx, key = sb("idx", [P, STEPS], U32), sb("key", [P, STEPS])
        wt = sb("w", [P, STEPS]) if weighted else None
        idx_st, key_st = sb("idx_st", [P, RINGS, U], U32), sb("key_st", [P, RINGS, U])
        w_st = sb("w_st", [P, RINGS, U]) if weighted else None
        rows = sb("rows", [P, RINGS, U, D])
        msg = sb("msg", [P, 2, U, D + 1]) if weighted else None
        oh = sb("oh", [P, 2, U, P])
        ps = ctx.enter_context(nc.psum_tensor(f"{name}_ps", [P, 2, U, P], F32))
        s_tab, s_staged, s_oh, s_msg, s_mm, s_acc, s_ones = [m.sem(f"{name}_{n}") for n in (
            "tables_in", "staged", "onehot_made", "msg_made", "summed", "added", "cleared")]
        s_rows = [m.sem(f"{name}_rows_in{r}") for r in range(RINGS)]
        NTAB = 3 if weighted else 2
        block = ctx.enter_context(nc.Block())

        @block.sync
        def _(sp):
            sp.dma_start(idx[:], idx_d).then_inc(s_tab, 16)
            sp.dma_start(key[:], m.key_d).then_inc(s_tab, 16)
            if weighted:
                sp.dma_start(wt[:], m.w_d).then_inc(s_tab, 16)

        @block.scalar
        def _(act):
            def stage(n, r, first):
                if not first:
                    act.wait_ge(s_rows[r], rows_in(n, r) - 16 * U)
                    act.wait_ge(s_oh, n - RINGS + 1)
                    if weighted:
                        act.wait_ge(s_msg, n - RINGS + 1)
                    alone(act)
                act.copy(idx_st[:, r, :], idx[:, bass.ds(n * U, U)])
                if weighted:
                    act.copy(w_st[:, r, :], wt[:, bass.ds(n * U, U)])
                act.copy(key_st[:, r, :], key[:, bass.ds(n * U, U)]).then_inc(s_staged, 1)

            def body(n, r, first, last):
                if not (last and r >= RINGS - 2):
                    stage(n + 2, (r + 2) % RINGS, first and r < 2)
                if weighted:
                    act.wait_ge(s_rows[r], rows_in(n, r))
                    if after(first, 2, r):
                        act.wait_ge(s_mm, n - 1)
                    for s in range(U):
                        ins = act.activation(msg[:, r % 2, s, 0:D], rows[:, r, s, :], ACT.Copy,
                                             scale=w_st[:, r, s:s + 1])
                    ins.then_inc(s_msg, 1)

            act.wait_ge(s_tab, 16 * NTAB)
            stage(0, 0, True)
            stage(1, 1, True)
            turns(act, body)

        @block.gpsimd
        def _(pool):
            def body(n, r, first, last):
                pool.wait_ge(s_staged, n + 1)
                if not first:
                    pool.wait_ge(s_msg if weighted else s_mm, n - RINGS + 1)
                alone(pool)
                for s in range(U):
                    pool.indirect_dma_start(rows[:, r, s, :], None, table,
                                            bass.IndirectOffsetOnAxis(idx_st[:, r, s:s + 1], 0)).then_inc(s_rows[r], 16)
            turns(pool, body)

        @block.tensor
        def _(pe):
            def body(n, r, first, last):
                pe.wait_ge(s_oh, n + 1)
                if weighted:
                    pe.wait_ge(s_msg, n + 1)
                else:
                    pe.wait_ge(s_rows[r], rows_in(n, r))
                if after(first, 2, r):
                    pe.wait_ge(s_acc, (n - 1) * U)
                for s in range(U):
                    ins = pe.matmul(ps[:, r % 2, s, 0:W], oh[:, r % 2, s, :],
                                    msg[:, r % 2, s, :] if weighted else rows[:, r, s, :], start=True, stop=True)
                ins.then_inc(s_mm, 1)
            if weighted:
                pe.wait_ge(s_ones, 2)
            turns(pe, body)

        @block.vector
        def _(dve):
            def add(n, r):
                dve.wait_ge(s_mm, n + 1)
                for s in range(U):
                    add_to_window(dve, m, ps[:, r % 2, s, 0:W], n * U + s, W, s_acc)

            def body(n, r, first, last):
                dve.wait_ge(s_staged, n + 1)
                if after(first, 2, r):
                    dve.wait_ge(s_mm, n - 1)
                onehots(dve, m, oh[:, r % 2], key_st[:, r], s_oh)
                if after(first, 1, r):
                    add(n - 1, (r - 1) % RINGS)

            dve.memset(m.acc[:], 0.0).then_inc(s_ones, 1)
            if weighted:
                dve.memset(msg[:, :, :, D:D + 1], 1.0).then_inc(s_ones, 1)
            dve.wait_ge(s_ones, 2 if weighted else 1)
            turns(dve, body)
            add(GROUPS - 1, RINGS - 1)
            dve.wait_ge(s_acc, GROUPS * U)


def rows_in(n, r, u=U):
    return (n - r) * (u * 16 // RINGS) + u * 16


def add_to_window(dve, m, part, k, W, s_acc):
    j = dve.value_load(m.winrow[0:1, bass.ds(k, 1)], min_val=0, max_val=WINS - 1)
    there = m.acc[:, bass.ds(j, 1), 0:W].rearrange("p o w -> p (o w)")
    if not (isinstance(k, int) and k == 0):
        dve.wait_ge(s_acc, k)
    dve.tensor_tensor(there, there, part, ALU.add).then_inc(s_acc, 1)


def load_nodes(eng, x_sb, x, sem):
    full = WINS - 1
    eng.dma_start(x_sb[:, 0:full, :], x[0:full * P, :].rearrange("(j p) d -> p j d", p=P)).then_inc(sem, 16)
    eng.dma_start(x_sb[0:TAIL, full, :], x[full * P:NODES, :]).then_inc(sem, 16)


class Norm:

    def __init__(self, sb):
        self.mean, self.var, self.rstd = sb("mean", [P, WINS]), sb("var", [P, WINS]), sb("rstd", [P, WINS])

    def stats(self, dve, link, y, sq, eps):
        link(dve.reduce_sum(self.mean[:], y, AX.X))
        link(dve.tensor_scalar(self.mean[:], self.mean[:], 1.0 / D, None, ALU.mult))
        link(dve.tensor_tensor(y, y, bc(self.mean[:], 2, D), ALU.subtract))
        link(dve.tensor_tensor(sq, y, y, ALU.mult))
        link(dve.reduce_sum(self.var[:], sq, AX.X))
        link(dve.tensor_scalar(self.var[:], self.var[:], 1.0 / D, eps, ALU.mult, ALU.add))

    STATS = 6

    def root(self, act):
        return act.activation(self.rstd[:], self.var[:], ACT.Sqrt)

    def scale(self, dve, link, y):
        link(dve.reciprocal(self.rstd[:], self.rstd[:]))
        link(dve.tensor_tensor(y, y, bc(self.rstd[:], 2, D), ALU.mult))

    SCALE = 2


def nodes_0(nc, m, x, Wt, b):
    with ExitStack() as ctx:
        def sb(n, shape, dt=F32):
            return ctx.enter_context(nc.sbuf_tensor(f"n0_{n}", shape, dt))

        w_sb, wT = sb("w_sb", [D, 2 * D]), sb("wT", [2 * D, D])
        b_sb = sb("b_sb", [P, D])
        cat, catT, h = sb("cat", [P, BLK, 2 * D]), sb("catT", [2 * D, BLK, P]), sb("h", [P, BLK, D])
        inv, sq = sb("inv", [P, WINS]), sb("sq", [P, WINS, D])
        norm = Norm(sb)
        pt = ctx.enter_context(nc.psum_tensor("n0_pt", [P, 8, P], F32))
        ph = ctx.enter_context(nc.psum_tensor("n0_ph", [P, 512], F32))
        s_in, s_dve, s_turned, s_catT, s_mm, s_wT, s_root, s_clear = [m.sem(f"n0_{n}") for n in (
            "in", "chain", "turned", "catT", "product", "wT", "root", "clear")]
        PER, PRE = 6, 3
        block = ctx.enter_context(nc.Block())

        @block.sync
        def _(sp):
            sp.dma_start(w_sb[:], Wt).then_inc(s_in, 16)
            sp.dma_start(b_sb[:], b.unsqueeze(0).broadcast_to([P, D])).then_inc(s_in, 16)
            sp.wait_ge(s_clear, 1)
            load_nodes(sp, m.x, x, s_in)

        @block.vector
        def _(dve):
            link = Link(dve, s_dve)
            dve.memset(m.x[:, WINS - 1, :], 0.0).then_inc(s_clear, 1)
            dve.wait_ge(s_wT, 1)
            link(dve.tensor_copy(wT[:], ph[:, 0:D]))
            link(dve.tensor_scalar(inv[:], m.acc[:, :, D:D + 1].rearrange("p j o -> p (j o)"), 1.0, None, ALU.max))
            link(dve.reciprocal(inv[:], inv[:]))
            assert link.n == PRE
            dve.wait_ge(s_in, 64)
            with dve.Fori(0, BLKS) as g:
                link.turn(PRE, g, PER)
                js = bass.ds(g * BLK, BLK)
                alone(dve)
                link(dve.tensor_copy(cat[:, :, 0:D], m.x[:, js, :]))
                link(dve.tensor_tensor(cat[:, :, D:2 * D], m.acc[:, js, 0:D], bc(inv[:, js], 2, D), ALU.mult))
                dve.wait_ge(s_mm, g + 1)
                link(dve.tensor_tensor(h[:], ph[:, 0:BLK * D].rearrange("p (j d) -> p j d", d=D), bc(b_sb[:], 1, BLK), ALU.add))
                link(dve.tensor_scalar(h[:], h[:], 0.0, None, ALU.max))
                link(dve.tensor_tensor(h[:], h[:], cat[:, :, 0:D], ALU.add))
                alone(dve)
                link(dve.tensor_copy(m.x[:, js, :], h[:]))
                assert link.n == PER
            link.turn(PRE + BLKS * PER, 0, 0)
            norm.stats(dve, link, m.x[:], sq[:], LN_EPS)
            dve.wait_ge(s_root, 1)
            norm.scale(dve, link, m.x[:])

        @block.tensor
        def _(pe):
            pe.wait_ge(s_in, 64)
            pe.transpose(ph[:, 0:D], w_sb[:], m.ident[0:D, 0:D]).then_inc(s_wT, 1)
            with pe.Fori(0, BLKS) as g:
                pe.wait_ge(s_dve, g * PER + PRE + 2)
                for j in range(BLK):
                    ins = pe.transpose(pt[:, j, :], cat[:, j, :], m.ident[:])
                ins.then_inc(s_turned, 1)
                pe.wait_ge(s_catT, g + 1)
                for j in range(BLK):
                    ins = pe.matmul(ph[:, j * D:(j + 1) * D], catT[:, j, :], wT[:], start=True, stop=True)
                ins.then_inc(s_mm, 1)

        @block.scalar
        def _(act):
            with act.Fori(0, BLKS) as g:
                act.wait_ge(s_turned, g + 1)
                act.copy(catT[:], pt[:, 0:BLK, :]).then_inc(s_catT, 1)
            act.wait_ge(s_dve, PRE + BLKS * PER + Norm.STATS)
            norm.root(act).then_inc(s_root, 1)


def put_nodes(nc, m, out):
    s_out = m.sem("nodes_out")
    with nc.Block() as block:
        @block.sync
        def _(sp):
            full = WINS - 1
            sp.dma_start(out[0:full * P, :].rearrange("(j p) d -> p j d", p=P), m.x[:, 0:full, :]).then_inc(s_out, 16)
            sp.dma_start(out[full * P:NODES, :], m.x[0:TAIL, full, :]).then_inc(s_out, 16)
            sp.wait_ge(s_out, 32)


ROW1 = D + HEADS
EF = 2 * HEADS


def edge_scores(nc, m, edge_attr, W, We, a):
    EP = 125
    E8 = P // EDIM
    C = EDGES // E8 // EP
    CH = 8
    assert EP * C * E8 == EDGES and C % CH == 0
    with ExitStack() as ctx:
        def sb(n, shape, dt=F32):
            return ctx.enter_context(nc.sbuf_tensor(f"es_{n}", shape, dt))

        w_sb, we_sb, we8, acol = sb("w", [D, D]), sb("we", [D, EDIM]), sb("we8", [D, E8, EDIM]), sb("acol", [D, 3])
        start, off, inside = sb("start", [P, E8]), sb("off", [P, E8]), sb("inside", [P, E8])
        a3 = sb("a3", [D, 3, HEADS])
        ve, bd = sb("ve", [P, HEADS]), sb("bd", [P, E8, HEADS])
        ea, eaT = sb("ea", [EP, 2, CH, P]), sb("eaT", [P, 2, CH, EP])
        se = sb("se", [EP, C, E8 * HEADS])
        pt = ctx.enter_context(nc.psum_tensor("es_pt", [P, 2, CH, P], F32))
        po = ctx.enter_context(nc.psum_tensor("es_po", [P, 2, 512], F32))
        pw = ctx.enter_context(nc.psum_tensor("es_pw", [P, 512], F32))
        s_w, s_dve, s_pw, s_turned, s_eaT, s_mm, s_se, s_out = [m.sem(f"es_{n}") for n in (
            "w_in", "chain", "w_products", "turned", "copied", "products", "scores", "out")]
        s_ea = [m.sem(f"es_in{b}") for b in range(2)]
        N = C // CH
        ea_v = edge_attr.rearrange("(p c e) i -> p c (e i)", p=EP, e=E8)
        block = ctx.enter_context(nc.Block())

        @block.sync
        def _(sp):
            sp.dma_start(w_sb[:], W.rearrange("h f i -> (h f) i")).then_inc(s_w, 16)
            sp.dma_start(we_sb[:], We.rearrange("h f i -> (h f) i")).then_inc(s_w, 16)
            with nc.allow_non_contiguous_dma(reason="192 weights, once"):
                for h in range(HEADS):
                    sp.dma_start(acol[h * HF:(h + 1) * HF, :], a[h].rearrange("(t f) -> f t", f=HF)).then_inc(s_w, 16)
            for b in range(2):
                sp.dma_start(ea[:, b], ea_v[:, b * CH:(b + 1) * CH, :]).then_inc(s_ea[b], 16)
            with sp.Fori(1, N // 2) as i:
                for b in range(2):
                    sp.wait_ge(s_turned, i * 2 + b - 1)
                    sp.dma_start(ea[:, b], ea_v[:, bass.ds(i * (2 * CH) + b * CH, CH), :]).then_inc(s_ea[b], 16)
            sp.wait_ge(s_se, N)
            sp.dma_start(m.se_d.rearrange("(p c e) h -> p (c e h)", p=EP, e=E8),
                         se[:].rearrange("p c k -> p (c k)")).then_inc(s_out, 16)
            sp.wait_ge(s_out, 16)

        @block.tensor
        def _(pe):
            pe.wait_ge(s_dve, 7)
            pe.transpose(pw[0:D, 0:D], w_sb[:], m.ident[0:D, 0:D])
            pe.matmul(pw[0:D, D:D + 2 * HEADS], w_sb[:], a3[:, 0:2, :].rearrange("p t h -> p (t h)"), start=True, stop=True)
            pe.matmul(pw[:, 256:256 + HEADS], we8[:].rearrange("p e i -> p (e i)"), a3[:, 2, :],
                      start=True, stop=True).then_inc(s_pw, 1)
            pe.wait_ge(s_dve, 10)

            def turn(n, b, first):
                pe.wait_ge(s_ea[b], (n - b) * 8 + 16)
                if not first:
                    pe.wait_ge(s_eaT, n - 1)
                for c in range(CH):
                    ins = pe.transpose(pt[:, b, c, 0:EP], ea[:, b, c, :], m.ident[0:EP, 0:EP])
                ins.then_inc(s_turned, 1)
                pe.wait_ge(s_eaT, n + 1)
                if not first:
                    pe.wait_ge(s_se, n - 1)
                for c in range(CH):
                    ins = pe.matmul(po[0:EP, b, c * E8 * HEADS:(c + 1) * E8 * HEADS], eaT[:, b, c, :],
                                    bd[:].rearrange("p e h -> p (e h)"), start=True, stop=True)
                ins.then_inc(s_mm, 1)
            for b in range(2):
                turn(b, b, True)
            with pe.Fori(1, N // 2) as i:
                for b in range(2):
                    turn(i * 2 + b, b, False)

        @block.scalar
        def _(act):
            def turn(n, b, first):
                act.wait_ge(s_turned, n + 1)
                if not first:
                    act.wait_ge(s_mm, n - 1)
                act.copy(eaT[:, b], pt[:, b, :, 0:EP]).then_inc(s_eaT, 1)
            for b in range(2):
                turn(b, b, True)
            with act.Fori(1, N // 2) as i:
                for b in range(2):
                    turn(i * 2 + b, b, False)

        @block.vector
        def _(dve):
            link = Link(dve, s_dve)
            link(dve.tensor_scalar(start[:], m.row[:, 0:E8], float(EDIM), None, ALU.mult))
            link(dve.tensor_scalar(off[:], start[:], m.col[:, 0:1], None, ALU.subtract))
            link(dve.tensor_scalar(inside[:], off[:], 0.0, None, ALU.is_le))
            link(dve.tensor_scalar(off[:], off[:], -float(EDIM), None, ALU.is_gt))
            link(dve.tensor_tensor(inside[:], inside[:], off[:], ALU.mult))
            dve.wait_ge(s_w, 16 * (2 + HEADS))
            for t in range(3):
                ins = dve.tensor_scalar(a3[:, t, :], inside[0:D, 0:HEADS], acol[:, t:t + 1], None, ALU.mult)
            link(ins)
            link(dve.tensor_copy(we8[:], bc(we_sb[:], 1, E8)))
            dve.wait_ge(s_pw, 1)
            link(dve.tensor_copy(m.rhs1[:], pw[0:D, 0:D + 2 * HEADS]))
            link(dve.tensor_copy(ve[:], pw[:, 256:256 + HEADS]))
            link(dve.tensor_tensor(bd[:], bc(ve[:], 1, E8), bc(inside[:], 2, HEADS), ALU.mult))
            with dve.Fori(0, N // 2) as i:
                for b in range(2):
                    n = i * 2 + b
                    dve.wait_ge(s_mm, n + 1)
                    alone(dve)
                    dve.tensor_copy(se[:, bass.ds(n * CH, CH), :],
                                    po[0:EP, b, 0:CH * E8 * HEADS].rearrange("p (c k) -> p c k", c=CH)).then_inc(s_se, 1)


def score_table(nc, m):
    with ExitStack() as ctx:
        def sb(n, shape, dt=F32):
            return ctx.enter_context(nc.sbuf_tensor(f"st_{n}", shape, dt))

        at, rows = sb("at", [QS, 2], U32), sb("rows", [QS, 2, P, HEADS])
        pt = ctx.enter_context(nc.psum_tensor("st_pt", [P, 2, HEADS, P], F32))
        s_at, s_turned, s_copied = [m.sem(f"st_{n}") for n in ("staged", "turned", "copied")]
        s_rows = [m.sem(f"st_rows{b}") for b in range(2)]
        se_v = m.se_d.rearrange("(t p) h -> t (p h)", p=P)
        block = ctx.enter_context(nc.Block())

        def pairs(eng, body):
            for b in range(2):
                body(b, b, True)
            with eng.Fori(1, GS // 2) as i:
                for b in range(2):
                    body(i * 2 + b, b, False)

        @block.scalar
        def _(act):
            def body(g, b, first):
                if not first:
                    act.wait_ge(s_turned, g - 1)
                    alone(act)
                act.copy(at[:, b:b + 1], m.tileq[:, bass.ds(g, 1)]).then_inc(s_at, 1)
            pairs(act, body)

        @block.gpsimd
        def _(pool):
            def body(g, b, first):
                pool.wait_ge(s_at, g + 1)
                if not first:
                    pool.wait_ge(s_turned, g - 1)
                alone(pool)
                pool.indirect_dma_start(rows[:, b].rearrange("q p h -> q (p h)"), None, se_v,
                                        bass.IndirectOffsetOnAxis(at[:, b:b + 1], 0)).then_inc(s_rows[b], 16)
            pairs(pool, body)

        @block.tensor
        def _(pe):
            def body(g, b, first):
                pe.wait_ge(s_rows[b], (g - b) * 8 + 16)
                if not first:
                    pe.wait_ge(s_copied, g - 1)
                for h in range(HEADS):
                    ins = pe.transpose(pt[:, b, h, 0:QS], rows[:, b, :, h], m.ident[0:QS, 0:QS])
                ins.then_inc(s_turned, 1)
            pairs(pe, body)

        @block.vector
        def _(dve):
            def body(g, b, first):
                dve.wait_ge(s_turned, g + 1)
                alone(dve)
                dve.tensor_copy(m.ef[:, bass.ds(g * QS, QS), 0:HEADS].rearrange("p q h -> p h q"),
                                pt[:, b, :, 0:QS]).then_inc(s_copied, 1)
            pairs(dve, body)


def table_1(nc, m):
    W = D + 2 * HEADS
    with ExitStack() as ctx:
        def sb(n, shape, dt=F32):
            return ctx.enter_context(nc.sbuf_tensor(f"t1_{n}", shape, dt))

        xT, tab = sb("xT", [D, BLK, P]), sb("tab", [P, WINS, W])
        pt = ctx.enter_context(nc.psum_tensor("t1_pt", [P, 8, P], F32))
        po = ctx.enter_context(nc.psum_tensor("t1_po", [P, 512], F32))
        s_xt, s_turned, s_xT, s_mm, s_tab, s_out = [m.sem(f"t1_{n}") for n in ("xt", "turned", "xT", "product", "tab", "out")]
        xt = sb("xt", [P, BLK, D])
        block = ctx.enter_context(nc.Block())

        @block.tensor
        def _(pe):
            with pe.Fori(0, BLKS) as g:
                pe.wait_ge(s_xt, g + 1)
                alone(pe)
                for j in range(BLK):
                    ins = pe.transpose(pt[0:D, j, :], xt[:, j, :], m.ident[:])
                ins.then_inc(s_turned, 1)
                pe.wait_ge(s_xT, g + 1)
                for j in range(BLK):
                    ins = pe.matmul(po[:, j * W:(j + 1) * W], xT[:, j, :], m.rhs1[:], start=True, stop=True)
                ins.then_inc(s_mm, 1)

        @block.scalar
        def _(act):
            with act.Fori(0, BLKS) as g:
                act.wait_ge(s_turned, g + 1)
                act.copy(xT[:], pt[0:D, 0:BLK, :]).then_inc(s_xT, 1)

        @block.vector
        def _(dve):
            def feed(g):
                dve.tensor_copy(xt[:], m.x[:, bass.ds(g * BLK, BLK), :]).then_inc(s_xt, 1)

            def take(g):
                dve.wait_ge(s_mm, g + 1)
                alone(dve)
                dve.tensor_copy(tab[:, bass.ds(g * BLK, BLK), :],
                                po[:, 0:BLK * W].rearrange("p (j w) -> p j w", w=W)).then_inc(s_tab, 1)
            feed(0)
            take(0)
            with dve.Fori(1, BLKS) as g:
                dve.wait_ge(s_turned, g)
                dve.wait_ge(s_tab, g)
                alone(dve)
                feed(g)
                take(g)
            dve.wait_ge(s_tab, BLKS)
            dve.tensor_copy(m.ssr[:], tab[:, :, D:W]).then_inc(s_tab, 1)

        @block.sync
        def _(sp):
            sp.wait_ge(s_tab, BLKS)
            sp.dma_start(m.t1_d.rearrange("(j p) w -> p j w", p=P), tab[:, :, 0:ROW1]).then_inc(s_out, 16)
            sp.wait_ge(s_out, 16)
            sp.wait_ge(s_tab, BLKS + 1)


def score_pass(nc, m):
    with ExitStack() as ctx:
        def sb(n, shape, dt=F32):
            return ctx.enter_context(nc.sbuf_tensor(f"sp_{n}", shape, dt))

        idx, key = sb("idx", [P, STEPS], U32), sb("key", [P, STEPS])
        idx_st, key_st = sb("idx_st", [P, RINGS, U], U32), sb("key_st", [P, RINGS, U])
        rows = sb("rows", [P, RINGS, U, ROW1])
        oh, ohT = sb("oh", [P, 2, U, P]), sb("ohT", [P, U, P])
        sc, void = sb("sc", [P, U, HEADS]), sb("void", [P, U])
        pt = ctx.enter_context(nc.psum_tensor("sp_pt", [P, 2, U, P], F32))
        pr = ctx.enter_context(nc.psum_tensor("sp_pr", [P, 2, 512], F32))
        s_tab, s_staged, s_oh, s_turned, s_ohT, s_mm, s_sc = [m.sem(f"sp_{n}") for n in (
            "tables_in", "staged", "onehot_made", "turned", "onehotT_made", "receiver", "scored")]
        s_rows = [m.sem(f"sp_rows_in{r}") for r in range(RINGS)]
        s_store = [m.sem(f"sp_stored{r}") for r in range(RINGS)]
        PER = 5
        block = ctx.enter_context(nc.Block())

        @block.sync
        def _(sp):
            sp.dma_start(idx[:], m.src_d).then_inc(s_tab, 16)
            sp.dma_start(key[:], m.key_d).then_inc(s_tab, 16)

            def body(n, r, first, last):
                sp.wait_ge(s_rows[r], rows_in(n, r))
                dst = m.g_d[n] if isinstance(n, int) else m.g_d[bass.ds(n, 1)].rearrange("o p w -> (o p) w")
                sp.dma_start(dst, rows[:, r].rearrange("p u w -> p (u w)")).then_inc(s_store[r], 16)
            turns(sp, body)
            for r in range(RINGS):
                sp.wait_ge(s_store[r], 16 * TURNS)

        @block.scalar
        def _(act):
            def stage(n, r, first):
                if not first:
                    act.wait_ge(s_rows[r], rows_in(n, r) - 16 * U)
                    act.wait_ge(s_sc, (n - RINGS + 1) * PER)
                    alone(act)
                act.copy(idx_st[:, r, :], idx[:, bass.ds(n * U, U)])
                act.copy(key_st[:, r, :], key[:, bass.ds(n * U, U)]).then_inc(s_staged, 1)

            def body(n, r, first, last):
                if not (last and r >= RINGS - 2):
                    stage(n + 2, (r + 2) % RINGS, first and r < 2)
                act.wait_ge(s_turned, n + 1)
                if after(first, 1, r):
                    act.wait_ge(s_mm, n)
                act.copy(ohT[:], pt[:, r % 2]).then_inc(s_ohT, 1)

            act.wait_ge(s_tab, 32)
            stage(0, 0, True)
            stage(1, 1, True)
            turns(act, body)

        @block.gpsimd
        def _(pool):
            def body(n, r, first, last):
                pool.wait_ge(s_staged, n + 1)
                if not first:
                    pool.wait_ge(s_sc, (n - RINGS + 1) * PER)
                    pool.wait_ge(s_store[r], (n - r) * (16 // RINGS))
                alone(pool)
                for s in range(U):
                    pool.indirect_dma_start(rows[:, r, s, :], None, m.t1_d,
                                            bass.IndirectOffsetOnAxis(idx_st[:, r, s:s + 1], 0)).then_inc(s_rows[r], 16)
            turns(pool, body)

        @block.tensor
        def _(pe):
            def body(n, r, first, last):
                pe.wait_ge(s_oh, n + 1)
                if after(first, 2, r):
                    pe.wait_ge(s_ohT, n - 1)
                for s in range(U):
                    ins = pe.transpose(pt[:, r % 2, s, :], oh[:, r % 2, s, :], m.ident[:])
                ins.then_inc(s_turned, 1)
                pe.wait_ge(s_ohT, n + 1)
                if after(first, 2, r):
                    pe.wait_ge(s_sc, (n - 1) * PER)
                for s in range(U):
                    j = pe.value_load(m.winrow[0:1, bass.ds(n * U + s, 1)], min_val=0, max_val=WINS - 1)
                    ins = pe.matmul(pr[:, r % 2, s * HEADS:(s + 1) * HEADS], ohT[:, s, :],
                                    m.ssr[:, bass.ds(j, 1), HEADS:2 * HEADS].rearrange("p o w -> p (o w)"),
                                    start=True, stop=True)
                ins.then_inc(s_mm, 1)
            turns(pe, body)

        @block.vector
        def _(dve):
            link = Link(dve, s_sc)

            def score(n, r):
                link.turn(0, n, PER)
                there = m.ef[:, bass.ds(n * U, U), 0:HEADS]
                dve.wait_ge(s_rows[r], rows_in(n, r))
                link(dve.tensor_tensor(sc[:], there, rows[:, r, :, D:ROW1], ALU.add))
                dve.wait_ge(s_mm, n + 1)
                link(dve.tensor_tensor(sc[:], sc[:], pr[:, r % 2, 0:U * HEADS].rearrange("p (u h) -> p u h", h=HEADS), ALU.add))
                link(dve.scalar_tensor_tensor(out=sc[:], in0=sc[:], scalar=0.01, in1=sc[:], op0=ALU.mult, op1=ALU.max))
                link(dve.tensor_scalar(void[:], key_st[:, r, :], 0.0, -BIG, ALU.is_lt, ALU.mult))
                link(dve.tensor_tensor(there, sc[:], bc(void[:], 2, HEADS), ALU.add))
                assert link.n == PER

            def body(n, r, first, last):
                dve.wait_ge(s_staged, n + 1)
                if after(first, 2, r):
                    dve.wait_ge(s_turned, n - 1)
                onehots(dve, m, oh[:, r % 2], key_st[:, r], s_oh)
                if after(first, 1, r):
                    score(n - 1, (r - 1) % RINGS)
            turns(dve, body)
            score(GROUPS - 1, RINGS - 1)



def steps_to_table(ap):
    return ap.rearrange("(g q) -> q g", q=QS)


def run_scans(dve, link, pen_st, pt, fw, bw, g, b, starts):
    for h in range(HEADS):
        f0, b0 = (-BIG, -BIG) if starts is None else [
            starts[:, d, h, bass.ds(g, 1)] for d in range(2)]
        dve.tensor_tensor_scan(fw[:, h, :], pen_st[:, b, 0:P],
                               pt[0:QS, b, h, :], f0, ALU.add, ALU.max)
        ins = dve.tensor_tensor_scan(bw[:, h, ::-1], pen_st[:, b, 1:P + 1][:, ::-1],
                                     pt[0:QS, b, h, ::-1], b0, ALU.add, ALU.max)
        link(ins)


def stage_scores(act, m, staged, pen, pen_st, g, b, s_staged):
    act.copy(pen_st[:, b, :], pen[:, bass.ds(g, 1), :].rearrange("q o p -> q (o p)"))
    act.copy(staged[:, b], m.ef[:, bass.ds(g * QS, QS), 0:HEADS].rearrange("p q h -> p h q")).then_inc(s_staged, 1)


def turn_scores(pe, m, staged, pt, g, b, s_staged, s_turned):
    pe.wait_ge(s_staged, g + 1)
    for h in range(HEADS):
        ins = pe.transpose(pt[0:QS, b, h, :], staged[:, b, h, :], m.ident[:])
    ins.then_inc(s_turned, 1)


def maxima_in_steps(nc, m):
    with ExitStack() as ctx:
        def sb(n, shape, dt=F32):
            return ctx.enter_context(nc.sbuf_tensor(f"ma_{n}", shape, dt))

        pen = sb("pen", [QS, GS, P + 1])
        fw, bw = sb("fw", [QS, HEADS, P]), sb("bw", [QS, HEADS, P])
        ends, whole = sb("ends", [QS, 2, HEADS, GS]), sb("whole", [QS, GS])
        staged, pen_st = sb("staged", [P, 2, HEADS, QS]), sb("pen_st", [QS, 2, P + 1])
        pt = ctx.enter_context(nc.psum_tensor("ma_pt", [P, 2, HEADS, P], F32))
        s_in, s_staged, s_turned, s_dve, s_out = [m.sem(f"ma_{n}") for n in ("pen_in", "staged", "turned", "chain", "out")]
        PER = HEADS + 2
        block = ctx.enter_context(nc.Block())

        @block.sync
        def _(sp):
            sp.dma_start(pen[:], m.pen_d.rearrange("g q p -> q g p")).then_inc(s_in, 16)
            sp.wait_ge(s_dve, 1 + GS * PER)
            with nc.allow_non_contiguous_dma(reason="one value a step and head"):
                for d in range(2):
                    for h in range(HEADS):
                        sp.dma_start(steps_to_table(m.ends_d[d, h]), ends[:, d, h, :]).then_inc(s_out, 16)
                sp.dma_start(steps_to_table(m.whole_d), whole[:]).then_inc(s_out, 16)
            sp.wait_ge(s_out, 16 * (2 * HEADS + 1))

        @block.tensor
        def _(pe):
            for b in range(2):
                turn_scores(pe, m, staged, pt, b, b, s_staged, s_turned)
            with pe.Fori(1, GS // 2) as i:
                for b in range(2):
                    pe.wait_ge(s_dve, (i * 2 + b - 1) * PER + 1)
                    turn_scores(pe, m, staged, pt, i * 2 + b, b, s_staged, s_turned)

        @block.scalar
        def _(act):
            act.wait_ge(s_in, 16)
            for b in range(2):
                stage_scores(act, m, staged, pen, pen_st, b, b, s_staged)
            with act.Fori(1, GS // 2) as i:
                for b in range(2):
                    act.wait_ge(s_dve, (i * 2 + b - 1) * PER + 1)
                    alone(act)
                    stage_scores(act, m, staged, pen, pen_st, i * 2 + b, b, s_staged)

        @block.vector
        def _(dve):
            link = Link(dve, s_dve)
            dve.wait_ge(s_in, 16)
            link(dve.tensor_reduce(whole[:], pen[:, :, 1:P], AX.X, ALU.min))
            with dve.Fori(0, GS // 2) as i:
                for b in range(2):
                    g = i * 2 + b
                    link.turn(1, g, PER)
                    dve.wait_ge(s_turned, g + 1)
                    alone(dve)
                    run_scans(dve, link, pen_st, pt, fw, bw, g, b, None)
                    for d, end in ((0, fw[:, :, P - 1]), (1, bw[:, :, 0])):
                        alone(dve)
                        link(dve.tensor_copy(ends[:, d, :, bass.ds(g, 1)].rearrange("q h o -> q (h o)"), end))
                    assert link.n == PER


def maxima_over_steps(nc, m):
    with ExitStack() as ctx:
        def sb(n, shape, dt=F32):
            return ctx.enter_context(nc.sbuf_tensor(f"mo_{n}", shape, dt))

        end, whole, both = sb("end", [HEADS, STEPS]), sb("whole", [HEADS, STEPS]), sb("both", [HEADS, STEPS])
        lnk, carry = sb("link", [HEADS, STEPS + 1]), sb("carry", [HEADS, STEPS + 1])
        s_in, s_end, s_dve, s_out = [m.sem(f"mo_{n}") for n in ("in", "ends_in", "chain", "out")]
        block = ctx.enter_context(nc.Block())

        def rows(ap):
            return ap.unsqueeze(0).broadcast_to([HEADS, STEPS])

        @block.sync
        def _(sp):
            sp.dma_start(lnk[:, 0:STEPS], rows(m.first_d)).then_inc(s_in, 16)
            sp.dma_start(both[:], rows(m.last_d)).then_inc(s_in, 16)
            sp.dma_start(whole[:], rows(m.whole_d)).then_inc(s_in, 16)
            sp.dma_start(end[:], m.ends_d[0]).then_inc(s_end, 16)
            sp.wait_ge(s_dve, 7)
            sp.dma_start(m.carry_d[0], carry[:]).then_inc(s_out, 16)
            sp.dma_start(m.link_d.unsqueeze(0), lnk[0:1, :]).then_inc(s_out, 16)
            sp.dma_start(end[:], m.ends_d[1]).then_inc(s_end, 16)
            sp.wait_ge(s_dve, 10)
            sp.wait_ge(s_out, 32)
            sp.dma_start(m.carry_d[1], carry[:]).then_inc(s_out, 16)
            sp.wait_ge(s_out, 48)

        @block.vector
        def _(dve):
            link = Link(dve, s_dve)
            dve.wait_ge(s_in, 48)
            link(dve.tensor_tensor(lnk[:, 1:STEPS], lnk[:, 1:STEPS], both[:, 0:STEPS - 1], ALU.not_equal))
            link(dve.tensor_scalar(lnk[:, 1:STEPS], lnk[:, 1:STEPS], -BIG, None, ALU.mult))
            dve.memset(lnk[:, 0:1], -BIG)
            link(dve.memset(lnk[:, STEPS:STEPS + 1], -BIG))
            link(dve.tensor_tensor(both[:], whole[:], lnk[:, 0:STEPS], ALU.add))
            link(dve.memset(carry[:, 0:1], -BIG))
            dve.wait_ge(s_end, 16)
            link(dve.tensor_tensor_scan(carry[:, 1:STEPS + 1], both[:], end[:], -BIG, ALU.add, ALU.max))
            link(dve.tensor_tensor(both[:], whole[:], lnk[:, 1:STEPS + 1], ALU.add))
            dve.wait_ge(s_end, 32)
            dve.wait_ge(s_out, 32)
            link(dve.memset(carry[:, STEPS:STEPS + 1], -BIG))
            link(dve.tensor_tensor_scan(carry[:, 0:STEPS][:, ::-1], both[:, ::-1], end[:, ::-1], -BIG, ALU.add, ALU.max))
            link(dve.tensor_copy(both[:, 0:1], both[:, 0:1]))


def weights(nc, m):
    with ExitStack() as ctx:
        def sb(n, shape, dt=F32):
            return ctx.enter_context(nc.sbuf_tensor(f"wt_{n}", shape, dt))

        pen = sb("pen", [QS, GS, P + 1])
        starts, lnk = sb("starts", [QS, 2, HEADS, GS]), sb("link", [QS, 2, GS])
        fw, bw, ex, end = sb("fw", [QS, HEADS, P]), sb("bw", [QS, HEADS, P]), sb("ex", [QS, HEADS, P]), sb("end", [QS, P])
        staged, pen_st = sb("staged", [P, 2, HEADS, QS]), sb("pen_st", [QS, 2, P + 1])
        pt = ctx.enter_context(nc.psum_tensor("wt_pt", [P, 2, HEADS, P], F32))
        pb = ctx.enter_context(nc.psum_tensor("wt_pb", [P, EF, P], F32))
        s_in, s_staged, s_turned, s_dve, s_exp, s_back = [m.sem(f"wt_{n}") for n in ("in", "staged", "turned", "chain", "exp", "turned_back")]
        PRE, PER = 2, HEADS + 5
        block = ctx.enter_context(nc.Block())

        @block.sync
        def _(sp):
            sp.dma_start(pen[:], m.pen_d.rearrange("g q p -> q g p")).then_inc(s_in, 16)
            with nc.allow_non_contiguous_dma(reason="one value a step and head"):
                for d in range(2):
                    sp.dma_start(lnk[:, d], steps_to_table(m.link_d[d:d + STEPS])).then_inc(s_in, 16)
                    for h in range(HEADS):
                        sp.dma_start(starts[:, d, h, :], steps_to_table(m.carry_d[d, h, d:d + STEPS])).then_inc(s_in, 16)

        @block.tensor
        def _(pe):
            def back(g):
                pe.wait_ge(s_dve, g * PER + PRE + HEADS + 4)
                pe.wait_ge(s_exp, g + 1)
                for h in range(HEADS):
                    pe.transpose(pb[:, h, 0:QS], ex[:, h, :], m.ident[0:QS, 0:QS])
                    ins = pe.transpose(pb[:, HEADS + h, 0:QS], fw[:, h, :], m.ident[0:QS, 0:QS])
                ins.then_inc(s_back, 1)

            def turn(g, b):
                turn_scores(pe, m, staged, pt, g, b, s_staged, s_turned)

            turn(0, 0)
            with pe.Fori(0, GS // 2 - 1) as i:
                turn(i * 2 + 1, 1)
                back(i * 2)
                turn(i * 2 + 2, 0)
                back(i * 2 + 1)
            turn(GS - 1, 1)
            back(GS - 2)
            back(GS - 1)

        @block.scalar
        def _(act):
            def exp(g):
                act.wait_ge(s_dve, g * PER + PRE + HEADS + 2)
                act.activation(ex[:], bw[:], ACT.Exp).then_inc(s_exp, 1)

            act.wait_ge(s_dve, PRE)
            for b in range(2):
                stage_scores(act, m, staged, pen, pen_st, b, b, s_staged)
            with act.Fori(0, GS // 2 - 1) as i:
                for b in range(2):
                    g = i * 2 + b
                    exp(g)
                    act.wait_ge(s_dve, g * PER + PRE + HEADS + 3)
                    alone(act)
                    stage_scores(act, m, staged, pen, pen_st, g + 2, b, s_staged)
            exp(GS - 2)
            exp(GS - 1)

        @block.vector
        def _(dve):
            link = Link(dve, s_dve)
            dve.wait_ge(s_in, 16 * (3 + 2 * HEADS))
            link(dve.tensor_copy(pen[:, :, 0], lnk[:, 0]))
            link(dve.tensor_copy(pen[:, :, P], lnk[:, 1]))
            with dve.Fori(0, GS // 2) as i:
                for b in range(2):
                    g = i * 2 + b
                    link.turn(PRE, g, PER)
                    dve.wait_ge(s_turned, g + 1)
                    alone(dve)
                    run_scans(dve, link, pen_st, pt, fw, bw, g, b, starts)
                    link(dve.tensor_tensor(fw[:], fw[:], bw[:], ALU.max))
                    link(dve.tensor_tensor(bw[:], pt[0:QS, b], fw[:], ALU.subtract))
                    link(dve.tensor_scalar(end[:], pen_st[:, b, 1:P + 1], 0.0, None, ALU.is_lt))
                    link(dve.tensor_tensor(fw[:], fw[:], bc(end[:], 1, HEADS), ALU.mult))
                    dve.wait_ge(s_back, g + 1)
                    alone(dve)
                    link(dve.tensor_copy(m.ef[:, bass.ds(g * QS, QS), :].rearrange("p q c -> p c q"), pb[:, :, 0:QS]))
                    assert link.n == PER


def attend_pass(nc, m):
    W = D + EF
    with ExitStack() as ctx:
        def sb(n, shape, dt=F32):
            return ctx.enter_context(nc.sbuf_tensor(f"ap_{n}", shape, dt))

        key = sb("key", [P, STEPS])
        key_st = sb("key_st", [P, RINGS, U])
        rows, msg, oh = sb("rows", [P, RINGS, U, ROW1]), sb("msg", [P, 2, U, D + EF]), sb("oh", [P, 2, U, P])
        ps = ctx.enter_context(nc.psum_tensor("ap_ps", [P, 2, U, P], F32))
        s_tab, s_staged, s_oh, s_msg, s_mm, s_acc, s_clear, s_out = [m.sem(f"ap_{n}") for n in (
            "tables_in", "staged", "onehot_made", "msg_made", "summed", "added", "cleared", "out")]
        s_rows = [m.sem(f"ap_rows_in{r}") for r in range(RINGS)]
        block = ctx.enter_context(nc.Block())

        @block.sync
        def _(sp):
            sp.dma_start(key[:], m.key_d).then_inc(s_tab, 16)

            def body(n, r, first, last):
                if not first:
                    sp.wait_ge(s_msg, n - RINGS + 1)
                src = m.g_d[n] if isinstance(n, int) else m.g_d[bass.ds(n, 1)].rearrange("o p w -> (o p) w")
                sp.dma_start(rows[:, r].rearrange("p u w -> p (u w)"), src).then_inc(s_rows[r], 16)
            turns(sp, body)
            sp.wait_ge(s_acc, GROUPS * U)
            sp.dma_start(m.acc_d, m.acc[:]).then_inc(s_out, 16)
            sp.wait_ge(s_out, 16)

        @block.scalar
        def _(act):
            def body(n, r, first, last):
                if not first:
                    act.wait_ge(s_oh, n - RINGS + 1)
                if after(first, 2, r):
                    act.wait_ge(s_mm, n - 1)
                    alone(act)
                act.copy(msg[:, r % 2, :, D:W], m.ef[:, bass.ds(n * U, U), :])
                act.copy(key_st[:, r, :], key[:, bass.ds(n * U, U)]).then_inc(s_staged, 1)
            act.wait_ge(s_tab, 16)
            turns(act, body)

        @block.tensor
        def _(pe):
            def body(n, r, first, last):
                pe.wait_ge(s_oh, n + 1)
                pe.wait_ge(s_msg, n + 1)
                if after(first, 2, r):
                    pe.wait_ge(s_acc, (n - 1) * U)
                for s in range(U):
                    ins = pe.matmul(ps[:, r % 2, s, 0:W], oh[:, r % 2, s, :], msg[:, r % 2, s, :], start=True, stop=True)
                ins.then_inc(s_mm, 1)
            turns(pe, body)

        @block.vector
        def _(dve):
            def add(n, r):
                dve.wait_ge(s_mm, n + 1)
                for s in range(U):
                    add_to_window(dve, m, ps[:, r % 2, s, 0:W], n * U + s, W, s_acc)

            def body(n, r, first, last):
                dve.wait_ge(s_staged, n + 1)
                onehots(dve, m, oh[:, r % 2], key_st[:, r], s_oh)
                dve.wait_ge(s_rows[r], (n - r) * (16 // RINGS) + 16)
                dve.tensor_tensor(msg[:, r % 2, :, 0:D].rearrange("p u (h f) -> p u h f", h=HEADS),
                                  rows[:, r, :, 0:D].rearrange("p u (h f) -> p u h f", h=HEADS),
                                  bc(msg[:, r % 2, :, D:D + HEADS], 3, HF), ALU.mult).then_inc(s_msg, 1)
                if after(first, 1, r):
                    add(n - 1, (r - 1) % RINGS)

            dve.memset(m.acc[:], 0.0).then_inc(s_clear, 1)
            dve.wait_ge(s_clear, 1)
            turns(dve, body)
            add(GROUPS - 1, RINGS - 1)


def nodes_1(nc, m, ln_scale, ln_bias):
    with ExitStack() as ctx:
        def sb(n, shape, dt=F32):
            return ctx.enter_context(nc.sbuf_tensor(f"n1_{n}", shape, dt))

        acc, wn, sq = sb("acc", [P, WINS, ACCW]), sb("wn", [P, WINS, D]), sb("sq", [P, WINS, D])
        own, low, none, top, fac, den = [sb(n, [P, WINS, HEADS]) for n in ("own", "low", "none", "top", "fac", "den")]
        gain, bias = sb("gain", [P, D]), sb("bias", [P, D])
        norm = Norm(sb)
        s_in, s_dve, s_act = [m.sem(f"n1_{n}") for n in ("in", "chain", "act")]
        block = ctx.enter_context(nc.Block())

        def heads(ap):
            return ap.rearrange("p j (h f) -> p j h f", h=HEADS)

        @block.sync
        def _(sp):
            sp.dma_start(acc[:], m.acc_d).then_inc(s_in, 16)
            sp.dma_start(wn[:], m.t1_d.rearrange("(j p) w -> p j w", p=P)[:, :, 0:D]).then_inc(s_in, 16)
            sp.dma_start(m.x[:], m.x_d).then_inc(s_in, 16)
            sp.dma_start(gain[:], ln_scale.unsqueeze(0).broadcast_to([P, D])).then_inc(s_in, 16)
            sp.dma_start(bias[:], ln_bias.unsqueeze(0).broadcast_to([P, D])).then_inc(s_in, 16)

        marks = []

        @block.vector
        def _(dve):
            link = Link(dve, s_dve)

            def hand():
                marks.append(link.n)
                dve.wait_ge(s_act, len(marks))

            dve.wait_ge(s_in, 80)
            link(dve.tensor_tensor(own[:], m.ssr[:, :, 0:HEADS], m.ssr[:, :, HEADS:], ALU.add))
            link(dve.scalar_tensor_tensor(out=own[:], in0=own[:], scalar=0.01, in1=own[:], op0=ALU.mult, op1=ALU.max))
            link(dve.tensor_scalar(none[:], acc[:, :, D:D + HEADS], 0.0, -BIG, ALU.is_le, ALU.mult))
            link(dve.tensor_tensor(low[:], acc[:, :, D + HEADS:], none[:], ALU.add))
            link(dve.tensor_tensor(top[:], low[:], own[:], ALU.max))
            link(dve.tensor_tensor(fac[:], low[:], top[:], ALU.subtract))
            link(dve.tensor_tensor(own[:], own[:], top[:], ALU.subtract))
            hand()
            link(dve.tensor_tensor(den[:], acc[:, :, D:D + HEADS], fac[:], ALU.mult))
            link(dve.tensor_tensor(den[:], den[:], own[:], ALU.add))
            link(dve.reciprocal(den[:], den[:]))
            link(dve.tensor_tensor(fac[:], fac[:], den[:], ALU.mult))
            link(dve.tensor_tensor(own[:], own[:], den[:], ALU.mult))
            link(dve.tensor_tensor(heads(sq[:]), heads(acc[:, :, 0:D]), bc(fac[:], 3, HF), ALU.mult))
            link(dve.tensor_tensor(heads(wn[:]), heads(wn[:]), bc(own[:], 3, HF), ALU.mult))
            link(dve.tensor_tensor(wn[:], wn[:], sq[:], ALU.add))
            link(dve.tensor_scalar(sq[:], wn[:], 0.0, None, ALU.min))
            hand()
            link(dve.tensor_scalar(wn[:], wn[:], 0.0, -1.0, ALU.max, ALU.add))
            link(dve.tensor_tensor(wn[:], wn[:], sq[:], ALU.add))
            norm.stats(dve, link, wn[:], sq[:], LN1_EPS)
            hand()
            norm.scale(dve, link, wn[:])
            link(dve.tensor_tensor(wn[:], wn[:], bc(gain[:], 1, WINS), ALU.mult))
            link(dve.tensor_tensor(wn[:], wn[:], bc(bias[:], 1, WINS), ALU.add))
            link(dve.tensor_tensor(m.x[:], m.x[:], wn[:], ALU.add))
            norm.stats(dve, link, m.x[:], sq[:], LN_EPS)
            hand()
            norm.scale(dve, link, m.x[:])

        @block.scalar
        def _(act):
            act.wait_ge(s_dve, marks[0])
            act.activation(fac[:], fac[:], ACT.Exp)
            act.activation(own[:], own[:], ACT.Exp).then_inc(s_act, 1)
            act.wait_ge(s_dve, marks[1])
            act.activation(sq[:], sq[:], ACT.Exp).then_inc(s_act, 1)
            act.wait_ge(s_dve, marks[2])
            norm.root(act).then_inc(s_act, 1)
            act.wait_ge(s_dve, marks[3])
            norm.root(act).then_inc(s_act, 1)


def keep_nodes(nc, m):
    s_out = m.sem("kept")
    with nc.Block() as block:
        @block.sync
        def _(sp):
            sp.dma_start(m.x_d, m.x[:]).then_inc(s_out, 16)
            sp.wait_ge(s_out, 16)


def table_2(nc, m, weight):
    W = ETYPES * D
    with ExitStack() as ctx:
        def sb(n, shape, dt=F32):
            return ctx.enter_context(nc.sbuf_tensor(f"t2_{n}", shape, dt))

        w_sb = sb("w", [D, ETYPES, D])
        xt, xT, tab = sb("xt", [P, 2, D]), sb("xT", [D, 2, P]), sb("tab", [P, 2, W])
        pt = ctx.enter_context(nc.psum_tensor("t2_pt", [P, 2, 512], F32))
        po = ctx.enter_context(nc.psum_tensor("t2_po", [P, 2, W], F32))
        s_w, s_xt, s_turned, s_xT, s_mm, s_lo, s_hi = [m.sem(f"t2_{n}") for n in (
            "w_in", "xt", "turned", "xT", "product", "low_half", "high_half")]
        s_out = [m.sem(f"t2_out{b}") for b in range(2)]
        block = ctx.enter_context(nc.Block())

        def pairs(eng, body):
            for b in range(2):
                body(b, b, True)
            with eng.Fori(1, WINS // 2) as i:
                for b in range(2):
                    body(i * 2 + b, b, False)

        @block.sync
        def _(sp):
            sp.dma_start(w_sb[:], weight.rearrange("r i o -> i r o")).then_inc(s_w, 16)

            def body(j, b, first):
                sp.wait_ge(s_lo, j + 1)
                sp.wait_ge(s_hi, j + 1)
                dst = m.t2_d[j] if isinstance(j, int) else m.t2_d[bass.ds(j, 1)].rearrange("o p w -> (o p) w")
                sp.dma_start(dst, tab[:, b, :]).then_inc(s_out[b], 16)
            pairs(sp, body)
            for b in range(2):
                sp.wait_ge(s_out[b], 16 * (WINS // 2))

        @block.tensor
        def _(pe):
            def turn(j, b):
                pe.wait_ge(s_xt, j + 1)
                alone(pe)
                pe.transpose(pt[0:D, b, 0:P], xt[:, b, :], m.ident[:]).then_inc(s_turned, 1)

            def body(j, b, first):
                pe.wait_ge(s_xT, j + 1)
                if not first:
                    pe.wait_ge(s_lo, j - 1)
                    pe.wait_ge(s_hi, j - 1)
                alone(pe)
                for k in range(2):
                    ins = pe.matmul(po[:, b, k * 512:(k + 1) * 512], xT[:, b, :],
                                    w_sb[:].rearrange("i r o -> i (r o)")[:, k * 512:(k + 1) * 512], start=True, stop=True)
                ins.then_inc(s_mm, 1)
            pe.wait_ge(s_w, 16)
            turn(0, 0)
            turn(1, 1)
            body(0, 0, True)
            with pe.Fori(1, WINS // 2) as i:
                turn(i * 2, 0)
                body(i * 2 - 1, 1, False)
                turn(i * 2 + 1, 1)
                body(i * 2, 0, False)
            body(WINS - 1, 1, False)

        @block.scalar
        def _(act):
            def body(j, b, first):
                act.wait_ge(s_turned, j + 1)
                if not first:
                    act.wait_ge(s_mm, j - 1)
                alone(act)
                act.copy(xT[:, b, :], pt[0:D, b, 0:P]).then_inc(s_xT, 1)
                act.wait_ge(s_mm, j + 1)
                if not first:
                    act.wait_ge(s_out[b], (j - b) * 8)
                alone(act)
                act.copy(tab[:, b, 0:512], po[:, b, 0:512]).then_inc(s_lo, 1)
            pairs(act, body)

        @block.vector
        def _(dve):
            def feed(j, b, first):
                if not first:
                    dve.wait_ge(s_turned, j - 1)
                    alone(dve)
                dve.tensor_copy(xt[:, b, :], m.x[:, bass.ds(j, 1), :].rearrange("p o d -> p (o d)")).then_inc(s_xt, 1)

            def take(j, b, first):
                dve.wait_ge(s_mm, j + 1)
                if not first:
                    dve.wait_ge(s_out[b], (j - b) * 8)
                    alone(dve)
                dve.tensor_copy(tab[:, b, 512:W], po[:, b, 512:W]).then_inc(s_hi, 1)
            feed(0, 0, True)
            feed(1, 1, True)
            take(0, 0, True)
            feed(2, 0, False)
            take(1, 1, True)
            feed(3, 1, False)
            take(2, 0, False)
            with dve.Fori(2, WINS // 2) as i:
                feed(i * 2, 0, False)
                take(i * 2 - 1, 1, False)
                feed(i * 2 + 1, 1, False)
                take(i * 2, 0, False)
            take(WINS - 1, 1, False)


def nodes_2(nc, m):
    with ExitStack() as ctx:
        def sb(n, shape, dt=F32):
            return ctx.enter_context(nc.sbuf_tensor(f"n2_{n}", shape, dt))

        sq, norm = sb("sq", [P, WINS, D]), Norm(sb)
        s_dve, s_root = m.sem("n2_chain"), m.sem("n2_root")
        block = ctx.enter_context(nc.Block())

        @block.vector
        def _(dve):
            link = Link(dve, s_dve)
            link(dve.tensor_tensor(m.x[:], m.x[:], m.acc[:, :, 0:D], ALU.add))
            norm.stats(dve, link, m.x[:], sq[:], LN_EPS)
            dve.wait_ge(s_root, 1)
            norm.scale(dve, link, m.x[:])

        @block.scalar
        def _(act):
            act.wait_ge(s_dve, 1 + Norm.STATS)
            norm.root(act).then_inc(s_root, 1)


U3 = 4
GROUPS3 = STEPS // U3
TURNS3 = GROUPS3 // RINGS
assert TURNS3 * RINGS * U3 == STEPS
COPIES = U3
SUMW = HEADS3 * D + HEADS3
XS = D + 2 * HEADS3
SUMROWS = NPAD + P


def table_3(nc, m, W, a):
    V = 2 * HEADS3
    with ExitStack() as ctx:
        def sb(n, shape, dt=F32):
            return ctx.enter_context(nc.sbuf_tensor(f"t3_{n}", shape, dt))

        wT, aT, v = sb("wT", [D, HEADS3]), sb("aT", [D, 2, HEADS3]), sb("v", [D, 2, HEADS3])
        xt, xT = sb("xt", [P, BLK, D]), sb("xT", [D, BLK, P])
        zeros = sb("zeros", [P, SUMROWS // P * SUMW])
        pt = ctx.enter_context(nc.psum_tensor("t3_pt", [P, 8, P], F32))
        po = ctx.enter_context(nc.psum_tensor("t3_po", [P, 512], F32))
        s_w, s_v, s_zero, s_xt, s_turned, s_xT, s_mm, s_tab, s_out = [m.sem(f"t3_{n}") for n in (
            "w_in", "v", "zero", "xt", "turned", "xT", "product", "tab", "out")]
        block = ctx.enter_context(nc.Block())

        @block.sync
        def _(sp):
            with nc.allow_non_contiguous_dma(reason="384 weights, once"):
                sp.dma_start(wT[:], W.rearrange("h d -> d h")).then_inc(s_w, 16)
                for t in range(2):
                    sp.dma_start(aT[:, t], a[:, (1 - t) * D:(2 - t) * D].rearrange("h d -> d h")).then_inc(s_w, 16)
            sp.wait_ge(s_zero, 1)
            for c in range(COPIES):
                sp.dma_start(m.sum_d[c].rearrange("(p j) w -> p (j w)", p=P), zeros[:]).then_inc(s_out, 16)
            sp.wait_ge(s_tab, BLKS + 1)
            with nc.allow_non_contiguous_dma(reason="two scores a node"):
                sp.dma_start(m.t3_d.rearrange("(j p) w -> p j w", p=P), m.xs[:, :, D + HEADS3:XS]).then_inc(s_out, 16)
            sp.wait_ge(s_out, 16 * (COPIES + 1))

        @block.gpsimd
        def _(pool):
            pool.memset(zeros[:], 0.0).then_inc(s_zero, 1)

        @block.tensor
        def _(pe):
            pe.wait_ge(s_v, 1)
            with pe.Fori(0, BLKS) as g:
                pe.wait_ge(s_xt, g + 1)
                alone(pe)
                for j in range(BLK):
                    ins = pe.transpose(pt[0:D, j, :], xt[:, j, :], m.ident[:])
                ins.then_inc(s_turned, 1)
                pe.wait_ge(s_xT, g + 1)
                for j in range(BLK):
                    ins = pe.matmul(po[:, j * V:(j + 1) * V], xT[:, j, :], v[:].rearrange("d t h -> d (t h)"), start=True, stop=True)
                ins.then_inc(s_mm, 1)

        @block.scalar
        def _(act):
            with act.Fori(0, BLKS) as g:
                act.wait_ge(s_turned, g + 1)
                act.copy(xT[:], pt[0:D, 0:BLK, :]).then_inc(s_xT, 1)

        @block.vector
        def _(dve):
            dve.wait_ge(s_w, 48)
            dve.tensor_tensor(v[:], aT[:], bc(wT[:], 1, 2), ALU.mult).then_inc(s_v, 1)

            def feed(g):
                dve.tensor_copy(xt[:], m.x[:, bass.ds(g * BLK, BLK), :]).then_inc(s_xt, 1)

            def take(g):
                dve.wait_ge(s_mm, g + 1)
                alone(dve)
                dve.tensor_copy(m.xs[:, bass.ds(g * BLK, BLK), D:XS],
                                po[:, 0:BLK * V].rearrange("p (j w) -> p j w", w=V)).then_inc(s_tab, 1)
            feed(0)
            take(0)
            with dve.Fori(1, BLKS) as g:
                dve.wait_ge(s_turned, g)
                dve.wait_ge(s_tab, g)
                alone(dve)
                feed(g)
                take(g)
            dve.tensor_copy(m.xs[:, :, 0:D], m.x[:]).then_inc(s_tab, 1)


def sum_by_src(nc, m):
    RW = D + HEADS3
    with ExitStack() as ctx:
        def sb(n, shape, dt=F32):
            return ctx.enter_context(nc.sbuf_tensor(f"s3_{n}", shape, dt))

        idx, key = sb("idx", [P, STEPS], U32), sb("key", [P, STEPS])
        idx_st, src_st, key_st = sb("idx_st", [P, RINGS, U3], U32), sb("src_st", [P, RINGS, U3]), sb("key_st", [P, RINGS, U3])
        rows = sb("rows", [P, RINGS, U3, HEADS3])
        valid, own, row, cnt, to = [sb(n, [P, RINGS, U3]) for n in ("valid", "own", "row", "cnt", "to")]
        put = sb("put", [P, RINGS, U3], U32)
        oh, ohT, same = sb("oh", [P, 2, U3, P]), sb("ohT", [P, 2, U3, P]), sb("same", [P, 2, U3, P])
        before = sb("before", [P, U3, P])
        sc, e_rows, sums = sb("sc", [P, 2, U3, HEADS3]), sb("e_rows", [P, 2, U3, SUMW]), sb("sums", [P, RINGS, U3, SUMW])
        pt = ctx.enter_context(nc.psum_tensor("s3_pt", [P, 2, U3, P], F32))
        pk = ctx.enter_context(nc.psum_tensor("s3_pk", [P, 2, U3, P], F32))
        pr = ctx.enter_context(nc.psum_tensor("s3_pr", [P, 2, U3, P], F32))
        ps = ctx.enter_context(nc.psum_tensor("s3_ps", [P, U3, 2 * P], F32))
        (s_tab, s_staged, s_row, s_oh, s_turned, s_ohT, s_rcv, s_same, s_put, s_sc, s_exp, s_erows, s_sum,
         s_sums) = [m.sem(f"s3_{n}") for n in (
            "tables_in", "staged", "row_chain", "onehot_made", "turned", "onehotT_made", "received", "same_made",
            "put_chain", "score_chain", "exp", "rows_made", "summed", "sums_made")]
        s_rows = [m.sem(f"s3_rows_in{r}") for r in range(RINGS)]
        s_add = [m.sem(f"s3_added{c}") for c in range(COPIES)]
        PROW, PPUT, PSC = 4, 2 + 3, 3
        block = ctx.enter_context(nc.Block())

        def walk(eng, body):
            turns(eng, body, TURNS3)

        def back(r, k):
            return (r - k) % RINGS

        @block.sync
        def _(sp):
            sp.dma_start(idx[:], m.src_d).then_inc(s_tab, 16)
            sp.dma_start(key[:], m.key_d).then_inc(s_tab, 16)
            for c in range(COPIES):
                sp.wait_ge(s_add[c], 16 * GROUPS3)

        @block.gpsimd
        def _(pool):
            def gather(n, r, first):
                pool.wait_ge(s_staged, n + 1)
                if not first:
                    pool.wait_ge(s_sc, (n - RINGS + 1) * PSC)
                alone(pool)
                for s in range(U3):
                    pool.indirect_dma_start(rows[:, r, s, :], None, m.t3_d,
                                            bass.IndirectOffsetOnAxis(idx_st[:, r, s:s + 1], 0)).then_inc(s_rows[r], 16)

            def scatter(n, r, first):
                pool.wait_ge(s_sums, n + 1)
                pool.wait_ge(s_put, (n + 1) * PPUT)
                for s in range(U3):
                    if not first:
                        pool.wait_ge(s_add[s], n * 16)
                    alone(pool)
                    pool.indirect_dma_start(m.sum_d[s], bass.IndirectOffsetOnAxis(put[:, r, s:s + 1], 0),
                                            sums[:, r, s, :], None, compute_op=ALU.add).then_inc(s_add[s], 16)

            def body(n, r, first, last):
                gather(n, r, first)
                if after(first, 3, r):
                    scatter(n - 3, back(r, 3), first and r == 3)
            walk(pool, body)
            for k in (3, 2, 1):
                scatter(GROUPS3 - k, back(0, k), False)

        @block.scalar
        def _(act):
            def stage(n, r, first):
                if not first:
                    act.wait_ge(s_rows[r], rows_in(n, r, U3) - 16 * U3)
                    act.wait_ge(s_sc, (n - RINGS + 1) * PSC)
                    alone(act)
                act.copy(idx_st[:, r, :], idx[:, bass.ds(n * U3, U3)])
                act.copy(src_st[:, r, :], idx[:, bass.ds(n * U3, U3)])
                act.copy(key_st[:, r, :], key[:, bass.ds(n * U3, U3)]).then_inc(s_staged, 1)

            def turn_out(n, r, first):
                act.wait_ge(s_turned, n + 1)
                if after(first, 2, r):
                    act.wait_ge(s_rcv, n - 1)
                act.copy(ohT[:, r % 2], pt[:, r % 2]).then_inc(s_ohT, 1)

            def exp(n, r, early):
                act.wait_ge(s_sc, (n + 1) * PSC)
                if not early:
                    act.wait_ge(s_sum, n - 1)
                act.activation(e_rows[:, r % 2, :, HEADS3 * D:SUMW], sc[:, r % 2], ACT.Exp).then_inc(s_exp, 1)

            def take(n, r, first):
                act.wait_ge(s_sum, n + 1)
                if not first:
                    for c in range(COPIES):
                        act.wait_ge(s_add[c], (n - RINGS + 1) * 16)
                act.copy(sums[:, r], ps[:, :, 0:SUMW]).then_inc(s_sums, 1)

            def body(n, r, first, last):
                if not (last and r >= RINGS - 2):
                    stage(n + 2, (r + 2) % RINGS, first and r < 2)
                turn_out(n, r, first)
                if after(first, 1, r):
                    exp(n - 1, back(r, 1), first and r < 3)
                if after(first, 2, r):
                    take(n - 2, back(r, 2), first)
            act.wait_ge(s_tab, 32)
            stage(0, 0, True)
            stage(1, 1, True)
            for r in range(RINGS):
                body(r, r, True, False)
            for r in range(RINGS):
                n = RINGS + r
                stage(n + 2, (r + 2) % RINGS, False)
                turn_out(n, r, False)
                exp(n - 1, back(r, 1), False)
                take(n - 2, back(r, 2), r < 2)
            with act.Fori(2, TURNS3 - 1) as i:
                for r in range(RINGS):
                    body(i * RINGS + r, r, False, False)
            for r in range(RINGS):
                body((TURNS3 - 1) * RINGS + r, r, False, True)
            exp(GROUPS3 - 1, RINGS - 1, False)
            take(GROUPS3 - 2, RINGS - 2, False)
            take(GROUPS3 - 1, RINGS - 1, False)

        @block.tensor
        def _(pe):
            def turn(n, r, first):
                pe.wait_ge(s_oh, n + 1)
                pe.wait_ge(s_row, (n + 1) * PROW)
                if after(first, 2, r):
                    pe.wait_ge(s_ohT, n - 1)
                    pe.wait_ge(s_same, n - 1)
                for s in range(U3):
                    pe.transpose(pt[:, r % 2, s, :], oh[:, r % 2, s, :], m.ident[:])
                for s in range(U3):
                    ins = pe.transpose(pk[:, r % 2, s, :], row[:, r, s:s + 1].to_broadcast([P, P]), m.ident[:])
                ins.then_inc(s_turned, 1)

            def receive(n, r, early):
                pe.wait_ge(s_ohT, n + 1)
                if not early:
                    pe.wait_ge(s_erows, n - 1)
                for s in range(U3):
                    j = pe.value_load(m.winrow[0:1, bass.ds(n * U3 + s, 1)], min_val=0, max_val=WINS - 1)
                    ins = pe.matmul(pr[:, r % 2, s, 0:RW], ohT[:, r % 2, s, :],
                                    m.xs[:, bass.ds(j, 1), 0:RW].rearrange("p o w -> p (o w)"), start=True, stop=True)
                ins.then_inc(s_rcv, 1)

            def sum_up(n, r, early):
                pe.wait_ge(s_erows, n + 1)
                pe.wait_ge(s_same, n + 1)
                if not early:
                    pe.wait_ge(s_sums, n)
                for s in range(U3):
                    ins = pe.matmul(ps[:, s, 0:SUMW], same[:, r % 2, s, :], e_rows[:, r % 2, s, :], start=True, stop=True)
                ins.then_inc(s_sum, 1)

            def body(n, r, first, last):
                turn(n, r, first)
                if after(first, 1, r):
                    receive(n - 1, back(r, 1), first and r < 3)
                if after(first, 2, r):
                    sum_up(n - 2, back(r, 2), first and r == 2)
            walk(pe, body)
            receive(GROUPS3 - 1, RINGS - 1, False)
            sum_up(GROUPS3 - 2, RINGS - 2, False)
            sum_up(GROUPS3 - 1, RINGS - 1, False)

        @block.vector
        def _(dve):
            la, lb, lc = Link(dve, s_row), Link(dve, s_put), Link(dve, s_sc)

            def rows_of(n, r, first):
                la.turn(0, n, PROW)
                dve.wait_ge(s_staged, n + 1)
                if not first:
                    dve.wait_ge(s_put, (n - RINGS + 1) * PPUT)
                la(dve.tensor_scalar(valid[:, r], key_st[:, r], 0.0, None, ALU.is_ge))
                la(dve.tensor_scalar(own[:, r], src_st[:, r], m.trash[:, 0:1], None, ALU.subtract))
                la(dve.tensor_tensor(own[:, r], own[:, r], valid[:, r], ALU.mult))
                la(dve.tensor_scalar(row[:, r], own[:, r], m.trash[:, 0:1], None, ALU.add))
                assert la.n == PROW
                if after(first, 2, r):
                    dve.wait_ge(s_turned, n - 1)
                onehots(dve, m, oh[:, r % 2], key_st[:, r], s_oh, U3)

            def match(n, r, first, early):
                dve.wait_ge(s_turned, n + 1)
                if not early:
                    dve.wait_ge(s_sum, n - 1)
                for s in range(U3):
                    ins = dve.tensor_scalar(same[:, r % 2, s, :], pk[:, r % 2, s, :], row[:, r, s:s + 1], None, ALU.is_equal)
                ins.then_inc(s_same, 1)
                dve.wait_ge(s_same, n + 1)
                lb.turn(0, n, PPUT)
                lb(dve.tensor_tensor(before[:], same[:, r % 2], bc(m.lower[:], 1, U3), ALU.mult))
                lb(dve.tensor_reduce(cnt[:, r], before[:], AX.X, ALU.max))
                lb(dve.tensor_scalar(cnt[:, r], cnt[:, r], 0.5, None, ALU.is_lt))
                lb(dve.tensor_tensor(to[:, r], own[:, r], cnt[:, r], ALU.mult))
                if not first:
                    for c in range(COPIES):
                        dve.wait_ge(s_add[c], (n - RINGS + 1) * 16)
                lb(dve.tensor_scalar(put[:, r], to[:, r], m.trash[:, 0:1], None, ALU.add))
                assert lb.n == PPUT
                lc.turn(0, n, PSC)
                dve.wait_ge(s_rows[r], rows_in(n, r, U3))
                dve.wait_ge(s_rcv, n + 1)
                if not early:
                    dve.wait_ge(s_exp, n - 1)
                lc(dve.tensor_tensor(sc[:, r % 2], pr[:, r % 2, :, D:RW], rows[:, r], ALU.add))
                lc(dve.scalar_tensor_tensor(out=sc[:, r % 2], in0=sc[:, r % 2], scalar=0.2, in1=sc[:, r % 2], op0=ALU.mult, op1=ALU.max))
                lc(dve.tensor_tensor(sc[:, r % 2], sc[:, r % 2], bc(valid[:, r], 2, HEADS3), ALU.mult))
                assert lc.n == PSC

            def weigh(n, r):
                dve.wait_ge(s_exp, n + 1)
                for h in range(HEADS3):
                    ins = dve.tensor_tensor(e_rows[:, r % 2, :, h * D:(h + 1) * D], pr[:, r % 2, :, 0:D],
                                            e_rows[:, r % 2, :, HEADS3 * D + h:HEADS3 * D + h + 1].broadcast_to([P, U3, D]), ALU.mult)
                ins.then_inc(s_erows, 1)

            def body(n, r, first, last):
                rows_of(n, r, first)
                if after(first, 1, r):
                    match(n - 1, back(r, 1), first, first and r < 3)
                if after(first, 2, r):
                    weigh(n - 2, back(r, 2))
            for r in range(RINGS):
                body(r, r, True, False)
            for r in range(RINGS):
                n = RINGS + r
                rows_of(n, r, False)
                match(n - 1, back(r, 1), r == 0, False)
                weigh(n - 2, back(r, 2))
            with dve.Fori(2, TURNS3 - 1) as i:
                for r in range(RINGS):
                    body(i * RINGS + r, r, False, False)
            for r in range(RINGS):
                body((TURNS3 - 1) * RINGS + r, r, False, True)
            match(GROUPS3 - 1, RINGS - 1, False, False)
            weigh(GROUPS3 - 2, RINGS - 2)
            weigh(GROUPS3 - 1, RINGS - 1)


def nodes_3(nc, m):
    with ExitStack() as ctx:
        def sb(n, shape, dt=F32):
            return ctx.enter_context(nc.sbuf_tensor(f"n3_{n}", shape, dt))

        tot, part = sb("tot", [P, WINS, SUMW]), sb("part", [P, WINS, SUMW])
        inv, pad = sb("inv", [P, WINS, HEADS3]), sb("pad", [P, 1])
        norm = Norm(sb)
        s_in, s_tot, s_dve, s_root = [m.sem(f"n3_{n}") for n in ("in", "part_in", "chain", "root")]
        sq = part[:, :, 0:D]
        block = ctx.enter_context(nc.Block())

        @block.sync
        def _(sp):
            def load(c, dst, sem):
                sp.dma_start(dst[:], m.sum_d[c][0:NPAD].rearrange("(j p) w -> p j w", p=P)).then_inc(sem, 16)
            load(0, tot, s_in)
            load(1, part, s_tot)
            for c in range(2, COPIES):
                sp.wait_ge(s_dve, c - 1)
                load(c, part, s_tot)

        @block.vector
        def _(dve):
            link = Link(dve, s_dve)
            dve.wait_ge(s_in, 16)
            for c in range(1, COPIES):
                dve.wait_ge(s_tot, 16 * c)
                link(dve.tensor_tensor(tot[:], tot[:], part[:], ALU.add))
            link(dve.tensor_scalar(pad[:], m.col[:], float(TAIL), None, ALU.is_ge))
            link(dve.tensor_scalar(tot[:, WINS - 1, HEADS3 * D:SUMW], tot[:, WINS - 1, HEADS3 * D:SUMW], pad[:, 0:1], None, ALU.add))
            link(dve.reciprocal(inv[:], tot[:, :, HEADS3 * D:SUMW]))
            link(dve.tensor_scalar(inv[:], inv[:], 1.0 / HEADS3, None, ALU.mult))
            for h in range(HEADS3):
                link(dve.tensor_tensor(tot[:, :, h * D:(h + 1) * D], tot[:, :, h * D:(h + 1) * D],
                                       inv[:, :, h:h + 1].broadcast_to([P, WINS, D]), ALU.mult))
                link(dve.tensor_tensor(m.x[:], m.x[:], tot[:, :, h * D:(h + 1) * D], ALU.add))
            norm.stats(dve, link, m.x[:], sq, LN_EPS)
            n_stats = link.n
            assert n_stats == COPIES - 1 + 4 + 2 * HEADS3 + Norm.STATS
            dve.wait_ge(s_root, 1)
            norm.scale(dve, link, m.x[:])

        @block.scalar
        def _(act):
            act.wait_ge(s_dve, COPIES - 1 + 4 + 2 * HEADS3 + Norm.STATS)
            norm.root(act).then_inc(s_root, 1)


def build(nc, x, src, dst, edge_attr, etype, w, W0, b0, W1, W1e, a1, s1, bb1, W2, W3, a3, out):
    with ExitStack() as ctx:
        m = Mem()
        m.sem = Semaphores(nc)

        def sb(name, shape, dt=F32):
            return ctx.enter_context(nc.sbuf_tensor(name, shape, dt))

        def dram(name, shape, dt=F32):
            return nc.dram_tensor(name, shape, dt, kind="Internal").ap()

        m.row, m.col, m.ident, m.lower, m.trash = sb("row", [P, P]), sb("col", [P, 1]), sb("ident", [P, P]), sb("lower", [P, P]), sb("trash", [P, 1])
        m.tileq, m.base, m.winrow = sb("tileq", [QS, GS], U32), sb("base", [QS, GS]), sb("winrow", [1, STEPS], I32)
        m.src_d, m.rel_d, m.w_d, m.key_d = [dram(n, [P, STEPS], dt) for n, dt in (
            ("src_d", U32), ("rel_d", U32), ("w_d", F32), ("key_d", F32))]
        m.pen_d, m.first_d, m.last_d = dram("pen_d", [GS, QS, P + 1]), dram("first_d", [STEPS]), dram("lastkey_d", [STEPS])
        constants(nc, m)
        schedule(nc, m, dst)
        step_tables(nc, m, src, dst, etype, w)
        m.t1_d, m.se_d, m.g_d = dram("t1_d", [NPAD, ROW1]), dram("se_d", [EDGES, HEADS]), dram("g_d", [GROUPS, P, U * ROW1])
        m.t2_d, m.t3_d = dram("t2_d", [WINS, P, ETYPES * D]), dram("t3_d", [NPAD, HEADS3])
        m.sum_d = [dram(f"sum_d{c}", [SUMROWS, SUMW]) for c in range(COPIES)]
        m.x_d, m.acc_d = dram("x_d", [P, WINS, D]), dram("acc_d", [P, WINS, ACCW])
        m.ends_d, m.whole_d = dram("ends_d", [2, HEADS, STEPS]), dram("whole_d", [STEPS])
        m.carry_d, m.link_d = dram("carry_d", [2, HEADS, STEPS + 1]), dram("link_d", [STEPS + 1])
        m.ssr, m.rhs1 = sb("ssr", [P, WINS, 2 * HEADS]), sb("rhs1", [D, D + 2 * HEADS])
        with nc.sbuf_tensor("x0", [P, WINS, D], F32) as m.x:
            with nc.sbuf_tensor("acc0", [P, WINS, ACCW], F32) as m.acc:
                sum_pass(nc, m, "l0", x, m.src_d, True)
                nodes_0(nc, m, x, W0, b0)
            edge_scores(nc, m, edge_attr, W1, W1e, a1)
            table_1(nc, m)
            keep_nodes(nc, m)
        with nc.sbuf_tensor("ef", [P, STEPS, EF], F32) as m.ef:
            score_table(nc, m)
            score_pass(nc, m)
            maxima_in_steps(nc, m)
            maxima_over_steps(nc, m)
            weights(nc, m)
            with nc.sbuf_tensor("acc1", [P, WINS, ACCW], F32) as m.acc:
                attend_pass(nc, m)
        with nc.sbuf_tensor("x1", [P, WINS, D], F32) as m.x:
            nodes_1(nc, m, s1, bb1)
            m.sem.clear()
            table_2(nc, m, W2)
            with nc.sbuf_tensor("acc2", [P, WINS, ACCW], F32) as m.acc:
                sum_pass(nc, m, "l2", m.t2_d.rearrange("j p (r o) -> (j p r) o", o=D), m.rel_d, False)
                nodes_2(nc, m)
            with nc.sbuf_tensor("xs", [P, WINS, XS], F32) as m.xs:
                table_3(nc, m, W3, a3)
                sum_by_src(nc, m)
            nodes_3(nc, m)
            put_nodes(nc, m, out)


_INS = ["x", "src", "dst", "edge_attr_16", "edge_type_16", "edge_weight1", "L0_gnn_W", "L0_gnn_b", "L1_gnn_W",
        "L1_gnn_W_edge", "L1_gnn_a", "L1_gnn_ln_scale", "L1_gnn_ln_bias", "L2_gnn_weight", "L3_gnn_W", "L3_gnn_a"]


def kernel(**inputs):
    import numpy as _np
    import concourse.bacc as _bacc
    from concourse import mybir as _mybir
    from concourse.bass_utils import run_bass_kernel_spmd as _run

    nc = _bacc.Bacc("TRN2", target_bir_lowering=False, num_devices=1)
    arrays, args = {}, []
    for name in _INS:
        a = _np.ascontiguousarray(inputs[name])
        arrays[f"in_{name}"] = a
        args.append(nc.dram_tensor(f"in_{name}", a.shape, _mybir.dt.from_np(a.dtype), kind="ExternalInput").ap())
    out = nc.dram_tensor("out_nodes", (NODES, D), F32, kind="ExternalOutput").ap()
    build(nc, *args, out)
    r = _run(nc, [arrays], core_ids=[0])
    return r.results[0]["out_nodes"]
```
